# Optimizing a Trainium2 kernel written in Bass

```python
import numpy as np
import jax
import jax.numpy as jnp

def _softmax(x, axis=-1):
    return jax.nn.softmax(x, axis=axis)

def _gelu(x):
    return jax.nn.gelu(x, approximate=True)

def _silu(x):
    return jax.nn.silu(x)

def _sigmoid(x):
    return jax.nn.sigmoid(x)

def _layernorm(x, axis=-1, eps=1e-05):
    m = jnp.mean(x, axis=axis, keepdims=True)
    v = jnp.var(x, axis=axis, keepdims=True)
    return (x - m) / jnp.sqrt(v + eps)

def _scatter_add(tgt, idx, src, axis=0):
    return tgt.at[idx].add(src)

def _segment_sum(src, seg, n):
    return jax.ops.segment_sum(src, seg, n)
kernel_name = 'mk_dlrm_tower_d1_rec_r8_3c3762'

def setup_inputs(seed: int=0):
    np.random.seed(seed)
    _w = jnp.asarray

    def _rec_inputs():
        import jax
        import jax.numpy as jnp
        _tk = jax.random.key(seed)
        ids = jnp.stack([jax.random.randint(jax.random.fold_in(_tk, 200 + f), (2048,), 0, v, jnp.int32) for f, v in enumerate([125000, 1250, 1250, 1250, 1250, 12500, 1000, 12500, 1000, 1250, 1000, 1000, 12500, 1250, 12500, 12500, 12500, 1000, 1250, 1000, 12500, 1000, 12500, 1250, 1250, 1000])], axis=1)
        tbl_0 = 0.05 * jax.random.normal(jax.random.fold_in(_tk, 500 + 0), (125000, 128), jnp.float32)
        tbl_1 = 0.05 * jax.random.normal(jax.random.fold_in(_tk, 500 + 1), (1250, 128), jnp.float32)
        tbl_2 = 0.05 * jax.random.normal(jax.random.fold_in(_tk, 500 + 2), (1250, 128), jnp.float32)
        tbl_3 = 0.05 * jax.random.normal(jax.random.fold_in(_tk, 500 + 3), (1250, 128), jnp.float32)
        tbl_4 = 0.05 * jax.random.normal(jax.random.fold_in(_tk, 500 + 4), (1250, 128), jnp.float32)
        tbl_5 = 0.05 * jax.random.normal(jax.random.fold_in(_tk, 500 + 5), (12500, 128), jnp.float32)
        tbl_6 = 0.05 * jax.random.normal(jax.random.fold_in(_tk, 500 + 6), (1000, 128), jnp.float32)
        tbl_7 = 0.05 * jax.random.normal(jax.random.fold_in(_tk, 500 + 7), (12500, 128), jnp.float32)
        tbl_8 = 0.05 * jax.random.normal(jax.random.fold_in(_tk, 500 + 8), (1000, 128), jnp.float32)
        tbl_9 = 0.05 * jax.random.normal(jax.random.fold_in(_tk, 500 + 9), (1250, 128), jnp.float32)
        tbl_10 = 0.05 * jax.random.normal(jax.random.fold_in(_tk, 500 + 10), (1000, 128), jnp.float32)
        tbl_11 = 0.05 * jax.random.normal(jax.random.fold_in(_tk, 500 + 11), (1000, 128), jnp.float32)
        tbl_12 = 0.05 * jax.random.normal(jax.random.fold_in(_tk, 500 + 12), (12500, 128), jnp.float32)
        tbl_13 = 0.05 * jax.random.normal(jax.random.fold_in(_tk, 500 + 13), (1250, 128), jnp.float32)
        tbl_14 = 0.05 * jax.random.normal(jax.random.fold_in(_tk, 500 + 14), (12500, 128), jnp.float32)
        tbl_15 = 0.05 * jax.random.normal(jax.random.fold_in(_tk, 500 + 15), (12500, 128), jnp.float32)
        tbl_16 = 0.05 * jax.random.normal(jax.random.fold_in(_tk, 500 + 16), (12500, 128), jnp.float32)
        tbl_17 = 0.05 * jax.random.normal(jax.random.fold_in(_tk, 500 + 17), (1000, 128), jnp.float32)
        tbl_18 = 0.05 * jax.random.normal(jax.random.fold_in(_tk, 500 + 18), (1250, 128), jnp.float32)
        tbl_19 = 0.05 * jax.random.normal(jax.random.fold_in(_tk, 500 + 19), (1000, 128), jnp.float32)
        tbl_20 = 0.05 * jax.random.normal(jax.random.fold_in(_tk, 500 + 20), (12500, 128), jnp.float32)
        tbl_21 = 0.05 * jax.random.normal(jax.random.fold_in(_tk, 500 + 21), (1000, 128), jnp.float32)
        tbl_22 = 0.05 * jax.random.normal(jax.random.fold_in(_tk, 500 + 22), (12500, 128), jnp.float32)
        tbl_23 = 0.05 * jax.random.normal(jax.random.fold_in(_tk, 500 + 23), (1250, 128), jnp.float32)
        tbl_24 = 0.05 * jax.random.normal(jax.random.fold_in(_tk, 500 + 24), (1250, 128), jnp.float32)
        tbl_25 = 0.05 * jax.random.normal(jax.random.fold_in(_tk, 500 + 25), (1000, 128), jnp.float32)
        _rk = jax.random.fold_in(_tk, 7)
        r_dense_features = -0.000520686 + 1.00062 * jax.random.normal(jax.random.fold_in(_rk, 101), (2048, 128), jnp.float32)
        W_top1 = 0.0405887 * jax.random.normal(jax.random.fold_in(_tk, 801), (607, 512), jnp.float32)
        W_top2 = 0.0441942 * jax.random.normal(jax.random.fold_in(_tk, 802), (512, 256), jnp.float32)
        W_top3 = 0.0625 * jax.random.normal(jax.random.fold_in(_tk, 803), (256, 1), jnp.float32)
        b_top1 = jnp.zeros((512,), jnp.float32)
        b_top2 = jnp.zeros((256,), jnp.float32)
        return (r_dense_features, ids, tbl_0, tbl_1, tbl_2, tbl_3, tbl_4, tbl_5, tbl_6, tbl_7, tbl_8, tbl_9, tbl_10, tbl_11, tbl_12, tbl_13, tbl_14, tbl_15, tbl_16, tbl_17, tbl_18, tbl_19, tbl_20, tbl_21, tbl_22, tbl_23, tbl_24, tbl_25, W_top1, b_top1, W_top2, b_top2, W_top3)
    r_dense_features, ids, tbl_0, tbl_1, tbl_2, tbl_3, tbl_4, tbl_5, tbl_6, tbl_7, tbl_8, tbl_9, tbl_10, tbl_11, tbl_12, tbl_13, tbl_14, tbl_15, tbl_16, tbl_17, tbl_18, tbl_19, tbl_20, tbl_21, tbl_22, tbl_23, tbl_24, tbl_25, W_top1, b_top1, W_top2, b_top2, W_top3 = _rec_inputs()

    def _L0_rec_setup():
        import jax, jax.numpy as jnp
        import numpy as np
        B, F, D = (2048, 26, 128)
        key = jax.random.key(seed)
        k1, k2 = jax.random.split(key)
        dense_features = jax.random.normal(k1, (B, D), dtype=jnp.float32)
        sparse_values = jax.random.normal(k2, (B, F, D), dtype=jnp.float32)
        return {'dense_features': dense_features, 'sparse_values': sparse_values}
    _L0_rec_all = _L0_rec_setup()
    _L0_rec_in = {k: v for k, v in _L0_rec_all.items() if k in ()}
    del _L0_rec_all
    return {'r_dense_features': r_dense_features, 'ids': ids, 'tbl_0': tbl_0, 'tbl_1': tbl_1, 'tbl_2': tbl_2, 'tbl_3': tbl_3, 'tbl_4': tbl_4, 'tbl_5': tbl_5, 'tbl_6': tbl_6, 'tbl_7': tbl_7, 'tbl_8': tbl_8, 'tbl_9': tbl_9, 'tbl_10': tbl_10, 'tbl_11': tbl_11, 'tbl_12': tbl_12, 'tbl_13': tbl_13, 'tbl_14': tbl_14, 'tbl_15': tbl_15, 'tbl_16': tbl_16, 'tbl_17': tbl_17, 'tbl_18': tbl_18, 'tbl_19': tbl_19, 'tbl_20': tbl_20, 'tbl_21': tbl_21, 'tbl_22': tbl_22, 'tbl_23': tbl_23, 'tbl_24': tbl_24, 'tbl_25': tbl_25, 'W_top1': W_top1, 'b_top1': b_top1, 'W_top2': W_top2, 'b_top2': b_top2, 'W_top3': W_top3}

def reference(r_dense_features, ids, tbl_0, tbl_1, tbl_2, tbl_3, tbl_4, tbl_5, tbl_6, tbl_7, tbl_8, tbl_9, tbl_10, tbl_11, tbl_12, tbl_13, tbl_14, tbl_15, tbl_16, tbl_17, tbl_18, tbl_19, tbl_20, tbl_21, tbl_22, tbl_23, tbl_24, tbl_25, W_top1, b_top1, W_top2, b_top2, W_top3):
    import jax
    import jax.numpy as jnp

    def _L0_rec_ref(dense_features, sparse_values):
        import jax, jax.numpy as jnp
        import numpy as np
        B, F, D = (2048, 26, 128)
        sd = jnp.einsum('bfd,bd->bf', sparse_values, dense_features)
        ss = jnp.einsum('bfd,bgd->bfg', sparse_values, sparse_values)
        iu, ju = jnp.triu_indices(F, k=1)
        pairs = ss[:, iu, ju]
        return jnp.concatenate([dense_features, sd, pairs], axis=1)
    e = jnp.stack([tbl_0[ids[:, 0]], tbl_1[ids[:, 1]], tbl_2[ids[:, 2]], tbl_3[ids[:, 3]], tbl_4[ids[:, 4]], tbl_5[ids[:, 5]], tbl_6[ids[:, 6]], tbl_7[ids[:, 7]], tbl_8[ids[:, 8]], tbl_9[ids[:, 9]], tbl_10[ids[:, 10]], tbl_11[ids[:, 11]], tbl_12[ids[:, 12]], tbl_13[ids[:, 13]], tbl_14[ids[:, 14]], tbl_15[ids[:, 15]], tbl_16[ids[:, 16]], tbl_17[ids[:, 17]], tbl_18[ids[:, 18]], tbl_19[ids[:, 19]], tbl_20[ids[:, 20]], tbl_21[ids[:, 21]], tbl_22[ids[:, 22]], tbl_23[ids[:, 23]], tbl_24[ids[:, 24]], tbl_25[ids[:, 25]]], axis=1)
    z = _L0_rec_ref(r_dense_features, e)
    z = z.reshape(z.shape[0], -1)
    h = jnp.concatenate([z, r_dense_features], axis=1)
    h = jnp.maximum(h @ W_top1 + b_top1, 0.0)
    h = jnp.maximum(h @ W_top2 + b_top2, 0.0)
    y = h @ W_top3
    return y

_drawn_inputs = setup_inputs


def setup_inputs(seed=0):
    import zlib

    import numpy as np

    out = dict(_drawn_inputs(seed))
    spreads = {'b_top1': (0.0, 0.1), 'b_top2': (0.0, 0.1)}
    factors = {}
    for name, (base, spread) in spreads.items():
        noise = np.random.default_rng([zlib.crc32(name.encode()), seed]).standard_normal(out[name].shape)
        drawn = base * np.exp(spread * noise) if base else spread * noise
        out[name] = jnp.asarray(drawn.astype(out[name].dtype))
    for name, factor in factors.items():
        out[name] = (out[name] * factor).astype(out[name].dtype)
    return out
```

```python
from contextlib import ExitStack

import concourse.bass as bass
from concourse import mybir

BATCH, TABLES, D = 2048, 26, 128
HALF, TILE, SPG = 256, 128, 4
JT = TILE // SPG
GPH = HALF // SPG
NHALF = BATCH // HALF
SLOTS = TABLES + 1
COLS = TABLES
ROWS = 32
PAIRS = TABLES * (TABLES + 1) // 2
FCH = 3
FK = PAIRS // FCH
H1, H2 = 512, 256
M1, M2 = H1 // 128, H2 // 128
HOT_ROWS = 1000
HOT_CH = 8
HOT_K = HOT_ROWS // HOT_CH
HOT = [6, 8, 10, 11, 17, 19, 21]
GATHERED = [t for t in range(TABLES) if t not in HOT]
ORDER = GATHERED + HOT
NG, NH = len(GATHERED), len(HOT)
TGROUPS = [list(range(a, min(a + 4, NG))) for a in range(0, NG, 4)]
GR = len(TGROUPS)
GB = JT // 4
UNITS = 2
HB = (NH + 1) // 2
RAW = 3

BACK, PAIR, LAYER1, LAYER2, LAYER3, USES = 0, 7, 9, 11, 12, 13
DRAINS = "vavavav" "vv" "aa" "a" "v"


def drained_before(i):
    return DRAINS[:i].count("v"), DRAINS[:i].count("a")


def width(c):
    return TABLES - c


def first_pair(c):
    return sum(width(i) for i in range(c))


def build(nc, ids_tiles, ids_hot, dense_t, tables, w1_dense, w1_pairs, b1, w2, b2, w3, y):
    fp32, f32r, i32 = mybir.dt.float32, mybir.dt.float32r, mybir.dt.int32
    ALU, ACT = mybir.AluOpType, mybir.ActivationFunctionType

    ctx = ExitStack()
    with ctx:
        def sb(name, shape, dt=fp32):
            return ctx.enter_context(nc.sbuf_tensor(name, shape, dt))

        def sem(name):
            return ctx.enter_context(nc.semaphore(name))

        ids_sb = sb("ids_sb", [128, 2 * NHALF + 2, TABLES], i32)
        index = sb("index", [128, 2, TABLES], i32)
        ids_cast = sb("ids_cast", [128, NH * HALF], i32)
        dense = sb("dense", [D, HALF])
        dense_hi, dense_lo = sb("dense_hi", [D, HALF], f32r), sb("dense_lo", [D, HALF], f32r)
        emb = sb("emb", [128, 2, NG * D])
        embT = sb("embT", [D, 2, JT, SPG, ROWS])
        onehot = sb("onehot", [128, UNITS, HOT_CH, HALF], f32r)
        hot_hi = sb("hot_hi", [HOT_K, NH, HOT_CH * D], f32r)
        hot_lo = sb("hot_lo", [HOT_K, NH, HOT_CH * D], f32r)
        row_id = sb("row_id", [128, HOT_CH])
        row_id_i = sb("row_id_i", [128, HOT_CH], i32)
        dots = sb("dots", [128, COLS, GPH])
        pairs_all = sb("pairs", [128, SPG, PAIRS])
        pairs = pairs_all[0:GPH, :, :]
        pairs_hi, pairs_lo = sb("pairs_hi", [FK, FCH, HALF], f32r), sb("pairs_lo", [FK, FCH, HALF], f32r)
        w1d_hi, w1d_lo = sb("w1d_hi", [128, H1], f32r), sb("w1d_lo", [128, H1], f32r)
        w1p_hi, w1p_lo = sb("w1p_hi", [FK, FCH * H1], f32r), sb("w1p_lo", [FK, FCH * H1], f32r)
        w2_hi, w2_lo = sb("w2_hi", [128, M1 * H2], f32r), sb("w2_lo", [128, M1 * H2], f32r)
        w3s = sb("w3s", [128, M2])
        b1s = sb("b1s", [128, M1])
        b2s = sb("b2s", [128, M2])
        h1 = sb("h1", [128, M1 * HALF])
        h1_hi, h1_lo = sb("h1_hi", [128, M1 * HALF], f32r), sb("h1_lo", [128, M1 * HALF], f32r)
        h2 = sb("h2", [128, M2, HALF])
        ys = sb("ys", [128, NHALF * 2])
        ident = sb("ident", [128, 128])
        scrap = sb("scrap", [1, 4])
        raw = [dots[:, :, :].rearrange("p c g -> p (c g)"), pairs_all[:, :, :].rearrange("p s f -> p (s f)"), h1]

        def bank(name):
            return ctx.enter_context(nc.psum_tensor(name, [128, 512], fp32))

        turn_ps = [bank(f"turn_ps{i}") for i in range(2)]
        hot_ps = [bank(f"hot_ps{i}") for i in range(2)]
        dots_ps = [bank(f"dots_ps{i}") for i in range(2)]
        misc_ps = [bank(f"misc_ps{i}") for i in range(2)]

        s_ids, s_out = sem("s_ids"), sem("s_out")
        s_consts = sem("s_consts")
        s_dense = sem("s_dense")
        s_cast = [sem(f"s_cast{i}") for i in range(2)]
        s_raw = [sem(f"s_raw{i}") for i in range(RAW)]
        s_fold = sem("s_fold")
        s_ident, s_rowid, s_rowid_f = sem("s_ident"), sem("s_rowid"), sem("s_rowid_f")
        split_hi, split_lo = sem("split_hi"), sem("split_lo")
        index_ready = [sem(f"index_ready{t}") for t in range(2)]
        gathered = [sem(f"gathered{t}") for t in range(2)]
        turn_full = sem("turn_full")
        turned = sem("turned")
        dense_in = sem("dense_in")
        dense_split_hi, dense_split = sem("dense_split_hi"), sem("dense_split")
        onehot_ready, hot_done = sem("onehot_ready"), sem("hot_done")
        hot_in = sem("hot_in")
        dots_full = sem("dots_full")
        dots_v, dots_a = sem("dots_v"), sem("dots_a")
        misc_full = sem("misc_full")
        misc_v, misc_a = sem("misc_v"), sem("misc_a")
        pairs_hi_ready = sem("pairs_hi_ready")
        h1_hi_ready, h1_ready = sem("h1_hi_ready"), sem("h1_ready")

        block = ctx.enter_context(nc.Block())

        def rows(slot, first, count):
            return embT[:, slot, :, :, first:first + count]

        def dots_part(t, b, s):
            at = t * JT + 4 * b
            return dots[32 * s:32 * s + 32, :, at:at + 4]

        def dots_bank(b, s):
            v = dots_ps[b % 2][32 * s:32 * s + 32, :].rearrange("p (g c) -> p c g", g=4)
            return v[:, s * 32:s * 32 + COLS, :]

        jobs = [(n % RAW, HOT_K, HOT_CH * D, hot_hi[:, n, :], hot_lo[:, n, :]) for n in range(NH)]
        jobs.append((2, 128, M1 * H2, w2_hi[:, :], w2_lo[:, :]))
        jobs.append((1, FK, 2 * H1, w1p_hi[:, 0:2 * H1], w1p_lo[:, 0:2 * H1]))
        jobs.append((2, FK, H1, w1p_hi[:, 2 * H1:3 * H1], w1p_lo[:, 2 * H1:3 * H1]))
        jobs.append((1, 128, H1, w1d_hi[:, :], w1d_lo[:, :]))
        NJ, FOLD = len(jobs), len(jobs) - 1

        def staged(eng, j):
            slot, parts, size = jobs[j][:3]
            eng.wait_ge(s_raw[slot], 16 * sum(job[0] == slot for job in jobs[:j + 1]))
            if j == FOLD:
                eng.wait_ge(s_fold, 1)
            return raw[slot][0:parts, 0:size]

        @block.sync
        def _(sp):
            def load_cast(part, half):
                a, b = (0, UNITS * HALF) if part == 0 else (UNITS * HALF, NH * HALF)
                src = ids_hot[bass.ds(half, 1), a:b]
                sp.dma_start(ids_cast[:, a:b], bass.AP(src.tensor, src.offset, [[0, 128], [1, b - a]]))\
                  .then_inc(s_cast[part], 16)

            def load_dense(half):
                sp.dma_start(dense[:, :], dense_t[bass.ds(half, 1), :, :].rearrange("a d n -> d (a n)"))\
                  .then_inc(s_dense, 16)

            sources = [tables[t].rearrange("(p c) d -> p (c d)", c=HOT_CH) for t in HOT]
            sources.append(w2.rearrange("(a p) n -> p a n", p=128))
            sources.append(w1_pairs[0:2 * FK, :].rearrange("(a p) n -> p a n", a=2))
            sources.append(w1_pairs[2 * FK:3 * FK, :])
            sources.append(w1_dense.rearrange("(a p) n -> p a n", a=2))

            def load_job(j):
                slot, parts, size = jobs[j][:3]
                before = [i for i in range(j) if jobs[i][0] == slot]
                if before:
                    sp.wait_ge(split_lo, before[-1] + 1)
                if j == NH:
                    sp.wait_ge(split_lo, NH)
                if j == FOLD:
                    size = 2 * H1
                out = raw[slot][0:parts, 0:size]
                if len(sources[j].shape) == 3:
                    out = out.rearrange("p (a n) -> p a n", a=sources[j].shape[1])
                sp.dma_start(out, sources[j]).then_inc(s_raw[slot], 16)

            sp.dma_start(ids_sb[:, 0:2 * NHALF, :], ids_tiles).then_inc(s_ids, 16)
            load_cast(0, 0)
            load_job(0)
            load_job(1)
            load_cast(1, 0)
            load_job(2)
            load_dense(0)
            sp.dma_start(w3s[:, :], w3).then_inc(s_consts, 16)
            sp.dma_start(b1s[:, :], b1).then_inc(s_consts, 16)
            sp.dma_start(b2s[:, :], b2).then_inc(s_consts, 16)
            for j in range(3, NH):
                load_job(j)
                if j == 3:
                    sp.wait_ge(onehot_ready, UNITS)
                    load_cast(0, 1)
            for j in range(NH, NJ):
                load_job(j)
            with sp.Fori(0, NHALF) as k:
                sp.wait_ge(onehot_ready, NH * (k + 1))
                load_cast(1, k + 1)
                sp.wait_ge(dense_split, k + 1)
                load_dense(k + 1)
                sp.wait_ge(onehot_ready, NH * (k + 1) + UNITS)
                load_cast(0, k + 2)
            sp.wait_ge(misc_v, DRAINS.count("v") * NHALF + 1)
            sp.dma_start(y, ys[:, :]).then_inc(s_out, 16)
            sp.wait_ge(s_out, 16)
            sp.wait_ge(s_cast[0], 16 * (NHALF + 2))
            sp.wait_ge(s_cast[1], 16 * (NHALF + 1))
            sp.wait_ge(s_dense, 16 * (NHALF + 1))

        @block.gpsimd
        def _(pool):
            pool.iota(row_id_i[:, :], [[1, HOT_CH]], base=0, channel_multiplier=HOT_CH).then_inc(s_rowid, 1)
            pool.memset(ident[:, :], 0.0).then_inc(s_ident, 1)
            pool.wait_ge(s_ident, 1)
            pool.affine_select(out=ident[:, :], in_=ident[:, :], compare_op=ALU.not_equal, fill=1.0,
                               base=0, pattern=[[-1, 128]], channel_multiplier=1).then_inc(s_ident, 1)
            with pool.Fori(0, NHALF) as k:
                for t in range(2):
                    pool.wait_ge(index_ready[t], k + 1)
                    pool.nop(nofuse=True)
                    for n, table in enumerate(GATHERED):
                        pool.indirect_dma_start(
                            emb[:, t, n * D:(n + 1) * D], None, tables[table],
                            bass.IndirectOffsetOnAxis(index[:, t, table:table + 1], 0)).then_inc(gathered[t], 16)

        @block.tensor
        def _(pe):
            def hot(k, n, first):
                b = n // 2
                if n % 2 == 0:
                    pe.wait_ge(hot_in, HB * k + b + 1)
                if first:
                    pe.wait_ge(split_lo, n + 1)
                pe.wait_ge(onehot_ready, NH * k + n + 1)
                out = hot_ps[b % 2][:, (n % 2) * HALF:(n % 2 + 1) * HALF]
                for c in range(HOT_CH):
                    for part in (hot_hi, hot_lo):
                        mm = nc.tensor.matmul(out, part[:, n, c * D:(c + 1) * D],
                                              onehot[0:HOT_K, n % UNITS, c, :],
                                              start=(c == 0 and part is hot_hi),
                                              stop=(c == HOT_CH - 1 and part is hot_lo))
                mm.then_inc(hot_done, 1)

            def turn(k, t, first, last):
                if first == 0:
                    pe.wait_ge(gathered[t], 16 * NG * (k + 1))
                for g, group in list(enumerate(TGROUPS))[first:last]:
                    u = t * GR + g
                    pe.wait_ge(turned, 2 * GR * k + u + 1)
                    for m, n in enumerate(group):
                        mm = nc.tensor.transpose(turn_ps[u % 2][:, m * 128:(m + 1) * 128],
                                                 emb[:, t, n * D:(n + 1) * D], ident[:, :])
                    mm.then_inc(turn_full, 1)

            def gram(k, t):
                pe.wait_ge(turned, 2 * GR * k + GR * (t + 1) + 2)
                pe.wait_ge(dense_in, k + 1)
                pe.wait_ge(hot_in, HB * (k + 1) + 2)
                for b in range(GB):
                    u = t * GB + b
                    pe.wait_ge(dots_v, 2 * GB * k + u + 1)
                    pe.wait_ge(dots_a, 2 * GB * k + u + 1)
                    for m in range(4):
                        group = embT[:, t, 4 * b + m, :, :]
                        out = dots_ps[b % 2][:, m * 128:(m + 1) * 128].rearrange("p (s c) -> p s c", s=SPG)
                        mm = nc.tensor.matmul(out[:, :, 0:COLS], group.rearrange("d s r -> d (s r)"),
                                              group[:, :, 0:COLS], start=True, stop=True)
                    mm.then_inc(dots_full, 1)

            def misc_bank(q, i):
                before = USES - 1 if i == 0 else USES - 2 if i == 1 else i - 2
                done = drained_before(before + 1)
                at = 1 if DRAINS[before] == "a" else 0
                n = DRAINS.count(DRAINS[before])
                pe.wait_ge((misc_v, misc_a)[at], n * q + (1 if i < 2 else done[at] + 1))
                return misc_ps[i % 2]

            def misc_drained(q, i):
                done = drained_before(i)
                pe.wait_ge(misc_v, DRAINS.count("v") * q + done[0] + 1)
                pe.wait_ge(misc_a, DRAINS.count("a") * q + done[1] + 1)

            def back(q, i):
                if i == 0:
                    pe.wait_ge(dots_v, 2 * GB * (q + 1) + 2)
                    pe.wait_ge(dots_a, 2 * GB * (q + 1) + 2)
                ps = misc_bank(q, BACK + i)
                pe.nop(nofuse=True)
                for m, c in enumerate(range(4 * i, min(4 * i + 4, COLS))):
                    mm = nc.tensor.transpose(ps[0:GPH, m * 128:(m + 1) * 128], dots[:, c, :], ident[:, :])
                mm.then_inc(misc_full, 1)

            def pair(q, i):
                if i == 0:
                    misc_drained(q, PAIR)
                ps = misc_bank(q, PAIR + i)
                pe.nop(nofuse=True)
                for f in range(2 * i, min(2 * i + 2, FCH)):
                    for s in range(SPG):
                        at = f % 2 * HALF + s * GPH
                        mm = nc.tensor.transpose(ps[0:FK, at:at + GPH], pairs[:, s, f * FK:(f + 1) * FK],
                                                 ident[0:GPH, 0:GPH])
                mm.then_inc(misc_full, 1)

            def split_product(out, chunks):
                terms = [term for w_hi, w_lo, x_hi, x_lo in chunks for term in ((w_hi, x_hi), (w_hi, x_lo), (w_lo, x_hi))]
                for n, (w, x) in enumerate(terms):
                    mm = nc.tensor.matmul(out, w, x, start=(n == 0), stop=(n == len(terms) - 1))
                return mm

            def layer1(q, i):
                if i == 0:
                    misc_drained(q, LAYER1)
                    pe.wait_ge(split_lo, NJ)
                    pe.wait_ge(dense_split, q + 1)
                ps = misc_bank(q, LAYER1 + i)
                for m in (2 * i, 2 * i + 1):
                    cols = slice(m * 128, (m + 1) * 128)
                    chunks = [(w1d_hi[:, cols], w1d_lo[:, cols], dense_hi[:, :], dense_lo[:, :])]
                    for f in range(FCH):
                        cols = slice(f * H1 + m * 128, f * H1 + (m + 1) * 128)
                        chunks.append((w1p_hi[:, cols], w1p_lo[:, cols], pairs_hi[:, f, :], pairs_lo[:, f, :]))
                    mm = split_product(ps[:, m % 2 * HALF:(m % 2 + 1) * HALF], chunks)
                mm.then_inc(misc_full, 1)

            def layer2(q, m):
                if m == 0:
                    pe.wait_ge(h1_ready, 2 * (q + 1))
                    misc_bank(q, LAYER2)
                ps = misc_ps[LAYER2 % 2]
                chunks = []
                for c in range(M1):
                    cols, x = slice(c * H2 + m * 128, c * H2 + (m + 1) * 128), slice(c * HALF, (c + 1) * HALF)
                    chunks.append((w2_hi[:, cols], w2_lo[:, cols], h1_hi[:, x], h1_lo[:, x]))
                mm = split_product(ps[:, m * HALF:(m + 1) * HALF], chunks)
                if m == M2 - 1:
                    mm.then_inc(misc_full, 1)

            def layer3(q):
                misc_drained(q, LAYER3)
                ps = misc_bank(q, LAYER3)
                for a in range(2):
                    for c in range(M2):
                        mm = nc.tensor.matmul(ps[:, a:a + 1], h2[:, c, a * 128:(a + 1) * 128], w3s[:, c:c + 1],
                                              start=(c == 0), stop=(c == M2 - 1))
                mm.then_inc(misc_full, 1)

            def half(k, first):
                q = None if first else k - 1
                for n in range(4):
                    hot(k, n, first)
                    if not first:
                        for i in range(2 * n, min(2 * n + 2, PAIR)):
                            back(q, i)
                turn(k, 0, 0, 2)
                hot(k, 4, first)
                turn(k, 0, 2, 4)
                if not first:
                    pair(q, 0)
                hot(k, 5, first)
                turn(k, 0, 4, GR)
                if not first:
                    pair(q, 1)
                if NH > 6:
                    hot(k, 6, first)
                if not first:
                    layer1(q, 0)
                if NH > 7:
                    hot(k, 7, first)
                if not first:
                    layer1(q, 1)
                gram(k, 0)
                turn(k, 1, 0, 2)
                if not first:
                    layer2(q, 0)
                turn(k, 1, 2, GR)
                if not first:
                    layer2(q, 1)
                gram(k, 1)
                if not first:
                    layer3(q)

            pe.wait_ge(s_ident, 2)
            half(0, True)
            pe.wait_ge(s_consts, 48)
            with pe.Fori(1, NHALF) as k:
                half(k, False)
            q = NHALF - 1
            for i in range(PAIR):
                back(q, i)
            for i in range(2):
                pair(q, i)
            for i in range(2):
                layer1(q, i)
            for m in range(M2):
                layer2(q, m)
            layer3(q)

        def misc_wait(eng, q, i):
            eng.wait_ge(misc_full, USES * q + i + 1)

        def back_out(eng, copy, q, i):
            misc_wait(eng, q, i)
            for m, c in enumerate(range(4 * i, min(4 * i + 4, COLS))):
                v = misc_ps[i % 2][0:GPH, m * 128:(m + 1) * 128].rearrange("g (s r) -> g s r", s=SPG)
                at = first_pair(c)
                last = copy(pairs[:, :, at:at + width(c)], v[:, :, c + 1:c + 1 + width(c)])
            last.then_inc(misc_v if DRAINS[i] == "v" else misc_a, 1)

        def pair_bank(i):
            w = (min(2 * i + 2, FCH) - 2 * i) * HALF
            return slice(2 * i * HALF, 2 * i * HALF + w), misc_ps[(PAIR + i) % 2][0:FK, 0:w]

        @block.scalar
        def _(act):
            def copy(out, in_):
                return nc.scalar.activation(out, in_, ACT.Copy)

            def split(j):
                data = staged(act, j)
                copy(jobs[j][3], data).then_inc(split_hi, 1)

            def hot_out(k, b):
                w = min(2, NH - 2 * b)
                act.wait_ge(hot_done, NH * k + 2 * b + w)
                for t in range(2):
                    v = hot_ps[b % 2][:, 0:w * HALF].rearrange("d (f t j s) -> d t j s f", f=w, t=2, j=JT)
                    out = copy(rows(t, 1 + NG + 2 * b, w), v[:, t])
                out.then_inc(hot_in, 1)

            def turn_out(k, t, first, last):
                for g, group in list(enumerate(TGROUPS))[first:last]:
                    u = t * GR + g
                    act.wait_ge(turn_full, 2 * GR * k + u + 1)
                    w = len(group)
                    v = turn_ps[u % 2][:, 0:w * 128].rearrange("d (f s j) -> d j s f", f=w, s=SPG)
                    copy(rows(t, 1 + group[0], w), v).then_inc(turned, 1)

            def dots_out(k, t, between={}):
                for b in range(GB):
                    if b in between:
                        between[b]()
                    act.wait_ge(dots_full, 2 * GB * k + t * GB + b + 1)
                    for s in (2, 3):
                        out = copy(dots_part(t, b, s), dots_bank(b, s))
                    out.then_inc(dots_a, 1)

            def pair_hi(q, i):
                misc_wait(act, q, PAIR + i)
                at, ps = pair_bank(i)
                copy(pairs_hi[:, :, :].rearrange("p f n -> p (f n)")[:, at], ps).then_inc(pairs_hi_ready, 1)

            def layer1_out(q, i):
                misc_wait(act, q, LAYER1 + i)
                for m in (2 * i, 2 * i + 1):
                    out = nc.scalar.activation(h1[:, m * HALF:(m + 1) * HALF],
                                               misc_ps[(LAYER1 + i) % 2][:, m % 2 * HALF:(m % 2 + 1) * HALF],
                                               ACT.Relu, bias=b1s[:, m:m + 1])
                out.then_inc(misc_a, 1)

            def layer1_hi(q, i):
                act.wait_ge(misc_a, DRAINS.count("a") * q + drained_before(LAYER1 + i + 1)[1] + 1)
                part = slice(2 * i * HALF, (2 * i + 2) * HALF)
                copy(h1_hi[:, part], h1[:, part]).then_inc(h1_hi_ready, 1)

            def layer2_out(q):
                misc_wait(act, q, LAYER2)
                for m in range(M2):
                    out = nc.scalar.activation(h2[:, m, :], misc_ps[LAYER2 % 2][:, m * HALF:(m + 1) * HALF],
                                               ACT.Relu, bias=b2s[:, m:m + 1])
                out.then_inc(misc_a, 1)

            def dense_hi_out(k):
                act.wait_ge(s_dense, 16 * (k + 1))
                copy(dense_hi[:, :], dense[:, :]).then_inc(dense_split_hi, 1)

            def half(k, first):
                q = None if first else k - 1
                for n in range(4):
                    if n % 2:
                        hot_out(k, n // 2)
                    if not first and 2 * n + 1 < PAIR:
                        back_out(act, copy, q, 2 * n + 1)
                turn_out(k, 0, 0, 4)
                if not first:
                    pair_hi(q, 0)
                turn_out(k, 0, 4, GR)
                hot_out(k, 2)
                if not first:
                    pair_hi(q, 1)
                if NH == 7:
                    hot_out(k, 3)
                if not first:
                    layer1_out(q, 0)
                    layer1_hi(q, 0)
                if NH == 8:
                    hot_out(k, 3)
                if not first:
                    layer1_out(q, 1)
                if first:
                    act.wait_ge(split_lo, NH)
                dots_out(k, 0, {1: lambda: first or layer1_hi(q, 1), 2: lambda: dense_hi_out(k)})
                if first:
                    for j in range(NH, NJ):
                        split(j)
                turn_out(k, 1, 0, GR)
                if not first:
                    layer2_out(q)
                dots_out(k, 1)

            for j in range(NH):
                split(j)
            act.wait_ge(s_consts, 48)
            half(0, True)
            with act.Fori(1, NHALF) as k:
                half(k, False)
            q = NHALF - 1
            for i in range(1, PAIR, 2):
                back_out(act, copy, q, i)
            for i in range(2):
                pair_hi(q, i)
            for i in range(2):
                layer1_out(q, i)
                layer1_hi(q, i)
            layer2_out(q)

        @block.vector
        def _(dve):
            def copy(out, in_):
                return nc.vector.tensor_copy(out, in_)

            def rest(out, full, high):
                return nc.vector.tensor_tensor(out, full, high, ALU.subtract)

            def split(j):
                data = staged(dve, j)
                dve.wait_ge(split_hi, j + 1)
                rest(jobs[j][4], data, jobs[j][3]).then_inc(split_lo, 1)

            def stage(t, tile):
                copy(index[:, t, :], ids_sb[:, bass.ds(tile, 1), :].rearrange("p a f -> p (a f)"))\
                    .then_inc(index_ready[t], 1)

            def stage_next(k, t):
                dve.wait_ge(turn_full, 2 * GR * k + GR * (t + 1))
                stage(t, 2 * k + t + 2)

            def one_hot(n, chunks=range(HOT_CH)):
                ids = ids_cast[0:HOT_K, n * HALF:(n + 1) * HALF]
                for c in chunks:
                    out = nc.vector.tensor_scalar(onehot[0:HOT_K, n % UNITS, c, :], ids, row_id[0:HOT_K, c:c + 1], None,
                                                  ALU.is_equal)
                if c == HOT_CH - 1:
                    out.then_inc(onehot_ready, 1)

            def one_hot_again(k, n):
                dve.wait_ge(hot_done, NH * k + n - UNITS + 1)
                one_hot(n)

            def dense_rows(k):
                dve.wait_ge(s_dense, 16 * (k + 1))
                for t in range(2):
                    v = dense[:, :].rearrange("d (s t j) -> d t j s", s=SPG, t=2)
                    out = copy(rows(t, 0, 1).rearrange("d j s r -> d j (s r)"), v[:, t])
                out.then_inc(dense_in, 1)

            def dots_out(k, t, ahead=False, between=None):
                for b in range(GB):
                    if between and b == 2:
                        between()
                    dve.wait_ge(dots_full, 2 * GB * k + t * GB + b + 1)
                    for s in (0, 1):
                        out = copy(dots_part(t, b, s), dots_bank(b, s))
                    out.then_inc(dots_v, 1)
                    if ahead:
                        if b == 0:
                            dve.wait_ge(hot_done, NH * (k + 1))
                        step = UNITS * HOT_CH // GB
                        one_hot(b * step // HOT_CH, range(b * step % HOT_CH, b * step % HOT_CH + step))

            def pair_lo(q, i):
                dve.wait_ge(pairs_hi_ready, 2 * q + i + 1)
                at, ps = pair_bank(i)
                rest(pairs_lo[:, :, :].rearrange("p f n -> p (f n)")[:, at], ps,
                     pairs_hi[:, :, :].rearrange("p f n -> p (f n)")[:, at]).then_inc(misc_v, 1)

            def h1_lo_out(q, i):
                dve.wait_ge(h1_hi_ready, 2 * q + i + 1)
                part = slice(2 * i * HALF, (2 * i + 2) * HALF)
                rest(h1_lo[:, part], h1[:, part], h1_hi[:, part]).then_inc(h1_ready, 1)

            def result(q):
                misc_wait(dve, q, LAYER3)
                copy(ys[:, bass.ds(2 * q, 2)], misc_ps[LAYER3 % 2][:, 0:2]).then_inc(misc_v, 1)

            def half(k, first):
                q = None if first else k - 1
                dense_rows(k)
                for n in range(2, 6):
                    if first:
                        split(n)
                    else:
                        back_out(dve, copy, q, 2 * n - 4)
                    one_hot_again(k, n)
                for n in (6, 7):
                    if first and n < NH:
                        split(n)
                    if n == 6 and n < NH:
                        one_hot_again(k, n)
                    if not first:
                        pair_lo(q, n - 6)
                    if n == 6:
                        stage_next(k, 0)
                    elif n < NH:
                        one_hot_again(k, n)
                if not first:
                    h1_lo_out(q, 0)
                dve.wait_ge(s_cast[0], 16 * (k + 2))

                def low_parts():
                    if not first:
                        h1_lo_out(q, 1)
                    dve.wait_ge(dense_split_hi, k + 1)
                    rest(dense_lo[:, :], dense[:, :], dense_hi[:, :]).then_inc(dense_split, 1)

                dots_out(k, 0, between=low_parts)
                if first:
                    for j in range(NH, NJ):
                        if j == FOLD:
                            dve.wait_ge(s_raw[jobs[j][0]], 16 * sum(job[0] == jobs[j][0] for job in jobs))
                            v = raw[jobs[j][0]]
                            nc.vector.tensor_tensor(v[:, 0:H1], v[:, 0:H1], v[:, H1:2 * H1], ALU.add).then_inc(s_fold, 1)
                        split(j)
                stage_next(k, 1)
                dots_out(k, 1, ahead=True)
                if not first:
                    result(q)

            nc.vector.memset(rows(0, SLOTS, ROWS - SLOTS), 0.0).then_inc(turned, 2)
            nc.vector.memset(rows(1, SLOTS, ROWS - SLOTS), 0.0).then_inc(hot_in, 2)
            nc.vector.memset(ids_sb[:, 2 * NHALF:, :], 0).then_inc(dots_v, 2)
            nc.vector.memset(scrap[:, 0:1], 0.0).then_inc(dots_a, 2)
            nc.vector.memset(scrap[:, 1:2], 0.0).then_inc(misc_v, 1)
            nc.vector.memset(scrap[:, 2:3], 0.0).then_inc(misc_a, 1)
            dve.wait_ge(s_ids, 16)
            for t in range(2):
                stage(t, t)
            dve.wait_ge(s_rowid, 1)
            copy(row_id[:, :], row_id_i[:, :]).then_inc(s_rowid_f, 1)
            dve.wait_ge(s_rowid_f, 1)
            dve.wait_ge(s_cast[0], 16)
            for n in range(UNITS):
                one_hot(n)
                split(n)
            dve.wait_ge(s_cast[1], 16)
            half(0, True)
            with dve.Fori(1, NHALF) as k:
                dve.wait_ge(s_cast[1], 16 * (k + 1))
                half(k, False)
            q = NHALF - 1
            for i in range(0, PAIR, 2):
                back_out(dve, copy, q, i)
            for i in range(2):
                pair_lo(q, i)
            for i in range(2):
                h1_lo_out(q, i)
            result(q)


def kernel(**inputs):
    import numpy as _np
    import concourse.bacc as _bacc
    from concourse import mybir as _mybir
    from concourse.bass_utils import run_bass_kernel_spmd as _run

    a = {name: _np.asarray(v) for name, v in inputs.items()}
    perm = []
    for c in range(COLS):
        for r in range(c + 1, SLOTS):
            if c == 0:
                perm.append(D + ORDER[r - 1])
            else:
                f, g = sorted((ORDER[c - 1], ORDER[r - 1]))
                perm.append(D + TABLES + f * (TABLES - 1) - f * (f - 1) // 2 + g - f - 1)
    w1 = a["W_top1"]
    ids = a["ids"].reshape(NHALF // 2, SPG, 2, 2, JT, TABLES)
    ids_tiles = ids.transpose(1, 4, 0, 2, 3, 5).reshape(TILE, 2 * NHALF, TABLES)
    ids_hot = ids[..., HOT].transpose(0, 2, 5, 3, 4, 1).reshape(NHALF, NH * HALF)
    dense = a["r_dense_features"].reshape(NHALF // 2, SPG, 2, GPH, D).transpose(0, 2, 4, 1, 3).reshape(NHALF, D, HALF)
    arrays = {
        "ids_tiles": ids_tiles,
        "ids_hot": _np.concatenate([ids_hot, ids_hot[:2]]),
        "dense_t": _np.concatenate([dense, dense[:1]]),
        "w1_dense": _np.concatenate([w1[:D], w1[-D:]]),
        "w1_pairs": w1[perm],
        "b1": a["b_top1"].reshape(-1, 128).T,
        "w2": a["W_top2"],
        "b2": a["b_top2"].reshape(-1, 128).T,
        "w3": a["W_top3"].reshape(-1, 128).T,
    }
    arrays.update({f"tbl_{t}": a[f"tbl_{t}"] for t in range(TABLES)})
    nc = _bacc.Bacc("TRN2", target_bir_lowering=False, num_devices=1)
    h = {}
    for name in arrays:
        arrays[name] = _np.ascontiguousarray(arrays[name])
        h[name] = nc.dram_tensor(name, arrays[name].shape, _mybir.dt.from_np(arrays[name].dtype), kind="ExternalInput").ap()
    y = nc.dram_tensor("y", (128, NHALF * 2), _mybir.dt.float32, kind="ExternalOutput").ap()
    build(nc, h["ids_tiles"], h["ids_hot"], h["dense_t"], [h[f"tbl_{t}"] for t in range(TABLES)], h["w1_dense"],
          h["w1_pairs"], h["b1"], h["w2"], h["b2"], h["w3"], y)
    r = _run(nc, [arrays], core_ids=[0])
    out = r.results[0]["y"].reshape(2, GPH, NHALF // 2, 2, 2)
    return _np.ascontiguousarray(out.transpose(2, 4, 0, 3, 1)).reshape(BATCH, 1)
```

```python
from contextlib import ExitStack

import concourse.bass as bass
from concourse import mybir

BATCH, TABLES, D = 2048, 26, 128
HALF, TILE, SPG = 256, 128, 4
JT = TILE // SPG
GPH = HALF // SPG
NHALF = BATCH // HALF
SLOTS = TABLES + 1
COLS = TABLES
ROWS = 32
PAIRS = TABLES * (TABLES + 1) // 2
CPAIRS = COLS // 2
MERGED = sum(TABLES - 1 - c for c in range(0, COLS, 2))
REST = MERGED - 128
POS = 128 + 64
FCH = 3
FK = [128, 128, 64 + REST]
H1, H2 = 512, 256
M1, M2 = H1 // 128, H2 // 128
HOT_ROWS = 1000
HOT_CH = 8
HOT_K = HOT_ROWS // HOT_CH
HOT = [6, 8, 10, 11, 17, 19, 21]
EARLY = 25
GATHERED = [t for t in range(TABLES) if t not in HOT + [EARLY]] + [EARLY]
ORDER = GATHERED + HOT
NG, NH = len(GATHERED), len(HOT)
TGROUPS = [list(range(a, min(a + 4, NG))) for a in range(0, NG, 4)]
GR = len(TGROUPS)
GB = JT // 4
UNITS = 3
HB = (NH + 1) // 2
TURNS = "a" * GR + "avavavav"[:GR]
RAW = 3

BACK, PAIR, LAYER1, LAYER2, LAYER3, USES = 0, 4, 6, 8, 9, 10
DRAINS = "aaaa" "vv" "aa" "a" "v"


def drained_before(i):
    return DRAINS[:i].count("v"), DRAINS[:i].count("a")


def turned_before(u):
    return TURNS[:u].count("v"), TURNS[:u].count("a")


def width(cp):
    return TABLES - 1 - 2 * cp


def first_merged(cp):
    return sum(width(i) for i in range(cp))


def build(nc, ids_tiles, ids_hot, ids_early, dense_t, tables, w1_dense, w1_pairs, b1, w2, b2, w3, y):
    fp32, f32r, i32 = mybir.dt.float32, mybir.dt.float32r, mybir.dt.int32
    ALU, ACT = mybir.AluOpType, mybir.ActivationFunctionType

    ctx = ExitStack()
    with ctx:
        def sb(name, shape, dt=fp32):
            return ctx.enter_context(nc.sbuf_tensor(name, shape, dt))

        def sem(name):
            return ctx.enter_context(nc.semaphore(name))

        ids_sb = sb("ids_sb", [128, 2 * NHALF + 2, TABLES], i32)
        index = sb("index", [128, 2, TABLES], i32)
        ids_cast = sb("ids_cast", [128, NH * HALF], i32)
        ids_cast_early = sb("ids_cast_early", [128, HALF], i32)
        dense = sb("dense", [D, HALF])
        dense_hi, dense_lo = sb("dense_hi", [D, HALF], f32r), sb("dense_lo", [D, HALF], f32r)
        emb = sb("emb", [128, 2, NG * D])
        embT = sb("embT", [D, 2, JT, SPG, ROWS])
        onehot = sb("onehot", [128, UNITS, HOT_CH, HALF], f32r)
        hot_hi = sb("hot_hi", [HOT_K, NH, HOT_CH * D], f32r)
        hot_lo = sb("hot_lo", [HOT_K, NH, HOT_CH * D], f32r)
        row_id = sb("row_id", [128, HOT_CH])
        row_id_i = sb("row_id_i", [128, HOT_CH], i32)
        dots = sb("dots", [128, COLS, GPH])
        pairs_all = sb("pairs_all", [128, HOT_CH * D])
        pairs = pairs_all[:, 0:SPG * POS].rearrange("p (s f) -> p s f", s=SPG)
        pairs_hi, pairs_lo = sb("pairs_hi", [128, FCH, HALF], f32r), sb("pairs_lo", [128, FCH, HALF], f32r)
        w1d_hi, w1d_lo = sb("w1d_hi", [128, H1], f32r), sb("w1d_lo", [128, H1], f32r)
        w1p_hi, w1p_lo = sb("w1p_hi", [128, FCH * H1], f32r), sb("w1p_lo", [128, FCH * H1], f32r)
        w2_hi, w2_lo = sb("w2_hi", [128, M1 * H2], f32r), sb("w2_lo", [128, M1 * H2], f32r)
        w3s = sb("w3s", [128, M2])
        b1s = sb("b1s", [128, M1])
        b2s = sb("b2s", [128, M2])
        h1 = sb("h1", [128, M1 * HALF])
        h1_hi, h1_lo = sb("h1_hi", [128, M1 * HALF], f32r), sb("h1_lo", [128, M1 * HALF], f32r)
        h2 = sb("h2", [128, M2, HALF])
        ys = sb("ys", [128, NHALF * 2])
        ident = sb("ident", [128, 128])
        early_hi, early_lo = h1_hi, h1_lo
        scrap = sb("scrap", [1, 4])
        raw = [dots[:, :, :].rearrange("p c g -> p (c g)"), pairs_all, h1]

        def bank(name):
            return ctx.enter_context(nc.psum_tensor(name, [128, 512], fp32))

        turn_ps = [bank(f"turn_ps{i}") for i in range(2)]
        hot_ps = [bank(f"hot_ps{i}") for i in range(2)]
        dots_ps = [bank(f"dots_ps{i}") for i in range(2)]
        misc_ps = [bank(f"misc_ps{i}") for i in range(2)]

        s_ids, s_out = sem("s_ids"), sem("s_out")
        s_consts = sem("s_consts")
        s_dense = sem("s_dense")
        s_cast = [sem(f"s_cast{i}") for i in range(2)]
        s_raw = [sem(f"s_raw{i}") for i in range(RAW)]
        s_fold = sem("s_fold")
        s_ident, s_rowid, s_rowid_f = sem("s_ident"), sem("s_rowid"), sem("s_rowid_f")
        split_hi, split_lo = sem("split_hi"), sem("split_lo")
        index_ready = [sem(f"index_ready{t}") for t in range(2)]
        gathered = [sem(f"gathered{t}") for t in range(2)]
        turn_full = sem("turn_full")
        turned_v, turned_a = sem("turned_v"), sem("turned_a")
        dense_in = sem("dense_in")
        dense_split_hi, dense_split = sem("dense_split_hi"), sem("dense_split")
        onehot_ready, hot_done = sem("onehot_ready"), sem("hot_done")
        s_cast_early, early_ready, early_done = sem("s_cast_early"), sem("early_ready"), sem("early_done")
        hot_in = sem("hot_in")
        dots_full = sem("dots_full")
        dots_v, dots_a = sem("dots_v"), sem("dots_a")
        misc_full = sem("misc_full")
        misc_v, misc_a = sem("misc_v"), sem("misc_a")
        pairs_hi_ready = sem("pairs_hi_ready")
        h1_hi_ready, h1_ready = sem("h1_hi_ready"), sem("h1_ready")

        end_full, end_v, end_a, end_hi, end_lo = (sem(f"end_{x}") for x in ("full", "v", "a", "hi", "lo"))
        END_BACK = misc_ps + turn_ps
        END_PAIR, END_LAYER1 = misc_ps, [ps[:, 0:HALF] for ps in hot_ps + dots_ps]
        END_LAYER2, END_LAYER3 = [ps[:, 0:HALF] for ps in turn_ps], misc_ps[0]
        END_H1, END_H2, END_Y = 2, 5, 6

        block = ctx.enter_context(nc.Block())

        def rows(slot, first, count):
            return embT[:, slot, :, :, first:first + count]

        def dots_part(t, b, s):
            at = t * JT + 4 * b
            return dots[32 * s:32 * s + 32, :, at:at + 4]

        def dots_bank(b, s):
            v = dots_ps[b % 2][32 * s:32 * s + 32, :].rearrange("p (g c) -> p c g", g=4)
            return v[:, s * 32:s * 32 + COLS, :]

        jobs = [(n % RAW, HOT_K, HOT_CH * D, hot_hi[:, n, :], hot_lo[:, n, :]) for n in range(NH)]
        jobs.append((NH % RAW, HOT_K, HOT_CH * D, early_hi[0:HOT_K, :], early_lo[0:HOT_K, :]))
        jobs.append((2, 128, M1 * H2, w2_hi[:, :], w2_lo[:, :]))
        jobs.append((1, 128, 2 * H1, w1p_hi[:, 0:2 * H1], w1p_lo[:, 0:2 * H1]))
        jobs.append((2, FK[2], H1, w1p_hi[0:FK[2], 2 * H1:3 * H1], w1p_lo[0:FK[2], 2 * H1:3 * H1]))
        jobs.append((1, 128, H1, w1d_hi[:, :], w1d_lo[:, :]))
        TJ, NJ, FOLD = NH + 1, len(jobs), len(jobs) - 1

        def staged(eng, j):
            slot, parts, size = jobs[j][:3]
            eng.wait_ge(s_raw[slot], 16 * sum(job[0] == slot for job in jobs[:j + 1]))
            if j == FOLD:
                eng.wait_ge(s_fold, 1)
            return raw[slot][0:parts, 0:size]

        @block.sync
        def _(sp):
            def load_cast(part, half):
                a, b = (0, UNITS * HALF) if part == 0 else (UNITS * HALF, NH * HALF)
                src = ids_hot[bass.ds(half, 1), a:b]
                sp.dma_start(ids_cast[:, a:b], bass.AP(src.tensor, src.offset, [[0, 128], [1, b - a]]))\
                  .then_inc(s_cast[part], 16)

            def load_dense(half):
                sp.dma_start(dense[:, :], dense_t[bass.ds(half, 1), :, :].rearrange("a d n -> d (a n)"))\
                  .then_inc(s_dense, 16)

            sources = [tables[t].rearrange("(p c) d -> p (c d)", c=HOT_CH) for t in HOT + [EARLY]]
            sources.append(w2.rearrange("(a p) n -> p a n", p=128))
            sources.append(w1_pairs[0:256, :].rearrange("(a p) n -> p a n", a=2))
            sources.append(w1_pairs[256:, :])
            sources.append(w1_dense.rearrange("(a p) n -> p a n", a=2))

            def load_job(j):
                slot, parts, size = jobs[j][:3]
                before = [i for i in range(j) if jobs[i][0] == slot]
                if before:
                    sp.wait_ge(split_lo, before[-1] + 1)
                if j == TJ:
                    sp.wait_ge(split_lo, TJ)
                if j == FOLD:
                    size = 2 * H1
                out = raw[slot][0:parts, 0:size]
                if len(sources[j].shape) == 3:
                    out = out.rearrange("p (a n) -> p a n", a=sources[j].shape[1])
                sp.dma_start(out, sources[j]).then_inc(s_raw[slot], 16)

            sp.dma_start(ids_sb[:, 0:2 * NHALF, :], ids_tiles).then_inc(s_ids, 16)
            load_cast(0, 0)
            load_job(0)
            load_job(1)
            load_cast(1, 0)
            load_job(2)
            load_dense(0)
            sp.dma_start(w3s[:, :], w3).then_inc(s_consts, 16)
            sp.dma_start(b1s[:, :], b1).then_inc(s_consts, 16)
            sp.dma_start(b2s[:, :], b2).then_inc(s_consts, 16)
            sp.dma_start(ids_cast_early[:, :], bass.AP(ids_early.tensor, ids_early.offset, [[0, 128], [1, HALF]]))\
              .then_inc(s_cast_early, 16)
            for j in range(3, TJ):
                load_job(j)
                if j == 3:
                    sp.wait_ge(onehot_ready, UNITS)
                    load_cast(0, 1)
            for j in range(TJ, NJ):
                load_job(j)
            with sp.Fori(0, NHALF) as k:
                sp.wait_ge(onehot_ready, NH * (k + 1))
                load_cast(1, k + 1)
                sp.wait_ge(dense_split, k + 1)
                load_dense(k + 1)
                sp.wait_ge(onehot_ready, NH * (k + 1) + UNITS)
                load_cast(0, k + 2)
            sp.wait_ge(end_v, END_Y)
            sp.dma_start(y, ys[:, :]).then_inc(s_out, 16)
            sp.wait_ge(s_out, 16)
            sp.wait_ge(s_cast[0], 16 * (NHALF + 2))
            sp.wait_ge(s_cast[1], 16 * (NHALF + 1))
            sp.wait_ge(s_dense, 16 * (NHALF + 1))

        @block.gpsimd
        def _(pool):
            pool.iota(row_id_i[:, :], [[1, HOT_CH]], base=0, channel_multiplier=HOT_CH).then_inc(s_rowid, 1)
            pool.memset(ident[:, :], 0.0).then_inc(s_ident, 1)
            pool.wait_ge(s_ident, 1)
            pool.affine_select(out=ident[:, :], in_=ident[:, :], compare_op=ALU.not_equal, fill=1.0,
                               base=0, pattern=[[-1, 128]], channel_multiplier=1).then_inc(s_ident, 1)

            def gather(k, t, tables_of_half):
                pool.wait_ge(index_ready[t], k + 1)
                pool.nop(nofuse=True)
                for n, table in enumerate(tables_of_half):
                    pool.indirect_dma_start(
                        emb[:, t, n * D:(n + 1) * D], None, tables[table],
                        bass.IndirectOffsetOnAxis(index[:, t, table:table + 1], 0)).then_inc(gathered[t], 16)

            for t in range(2):
                gather(0, t, GATHERED[:-1])
            with pool.Fori(1, NHALF) as k:
                for t in range(2):
                    gather(k, t, GATHERED)

        @block.tensor
        def _(pe):
            def hot(k, n, first):
                b = n // 2
                if n % 2 == 0:
                    pe.wait_ge(hot_in, HB * k + b + 1)
                if first:
                    pe.wait_ge(split_lo, n + 1)
                pe.wait_ge(onehot_ready, NH * k + n + 1)
                out = hot_ps[b % 2][:, (n % 2) * HALF:(n % 2 + 1) * HALF]
                look_up(out, hot_hi[:, n, :], hot_lo[:, n, :], n % UNITS).then_inc(hot_done, 1)

            def look_up(out, high, low, unit):
                for c in range(HOT_CH):
                    for part in (high, low):
                        mm = nc.tensor.matmul(out, part[:, c * D:(c + 1) * D], onehot[0:HOT_K, unit, c, :],
                                              start=(c == 0 and part is high),
                                              stop=(c == HOT_CH - 1 and part is low))
                return mm

            def early():
                b = NH // 2
                if NH % 2 == 0:
                    pe.wait_ge(hot_in, b + 1)
                pe.wait_ge(split_lo, TJ)
                pe.wait_ge(early_ready, 1)
                look_up(hot_ps[b % 2][:, HALF * (NH % 2):HALF * (NH % 2 + 1)], early_hi[0:HOT_K, :],
                        early_lo[0:HOT_K, :], NH % UNITS).then_inc(early_done, 1)

            def turn_drained(k, u):
                done, engine = turned_before(u % (2 * GR) + 1), TURNS[u]
                at, count = ("va".index(engine), TURNS.count(engine))
                pe.wait_ge((turned_v, turned_a)[at], count * (k - 1 if u < 0 else k) + done[at])

            def turn(k, t, first, last, is_first=False):
                if first == 0:
                    pe.wait_ge(gathered[t], 16 * (NG - 1) if is_first else 16 * NG * (k + 1) - 16)
                for g, group in list(enumerate(TGROUPS))[first:last]:
                    u = t * GR + g
                    if u >= 2 or not is_first:
                        turn_drained(k, u - 2)
                    for m, n in enumerate(group):
                        if is_first and n == NG - 1:
                            break
                        mm = nc.tensor.transpose(turn_ps[u % 2][:, m * 128:(m + 1) * 128],
                                                 emb[:, t, n * D:(n + 1) * D], ident[:, :])
                    mm.then_inc(turn_full, 1)

            def gram(k, t):
                done = turned_before(GR * (t + 1))
                if t == 1:
                    pe.wait_ge(turned_v, TURNS.count("v") * k + done[0])
                pe.wait_ge(turned_a, TURNS.count("a") * k + done[1])
                pe.wait_ge(dense_in, k + 1)
                pe.wait_ge(hot_in, HB * (k + 1) + 2)
                for b in range(GB):
                    u = t * GB + b
                    pe.wait_ge(dots_v, 2 * GB * k + u + 1)
                    pe.wait_ge(dots_a, 2 * GB * k + u + 1)
                    for m in range(4):
                        group = embT[:, t, 4 * b + m, :, :]
                        out = dots_ps[b % 2][:, m * 128:(m + 1) * 128].rearrange("p (s c) -> p s c", s=SPG)
                        mm = nc.tensor.matmul(out[:, :, 0:COLS], group.rearrange("d s r -> d (s r)"),
                                              group[:, :, 0:COLS], start=True, stop=True)
                    mm.then_inc(dots_full, 1)

            def misc_bank(q, i):
                before = (i - 2) % USES
                done = drained_before(before + 1)
                at = 1 if DRAINS[before] == "a" else 0
                n = DRAINS.count(DRAINS[before])
                pe.wait_ge((misc_v, misc_a)[at], n * q + (1 if i < 2 else done[at] + 1))
                return misc_ps[i % 2]

            def misc_drained(q, i):
                done = drained_before(i)
                pe.wait_ge(misc_v, DRAINS.count("v") * q + done[0] + 1)
                pe.wait_ge(misc_a, DRAINS.count("a") * q + done[1] + 1)

            def back(q, i):
                if i == 0:
                    pe.wait_ge(dots_v, 2 * GB * (q + 1) + 2)
                    pe.wait_ge(dots_a, 2 * GB * (q + 1) + 2)
                back_into(misc_bank(q, BACK + i), i).then_inc(misc_full, 1)

            def back_into(ps, i):
                for m, cp in enumerate(range(4 * i, min(4 * i + 4, CPAIRS))):
                    mm = nc.tensor.transpose(ps[:, m * 128:(m + 1) * 128],
                                             dots[:, 2 * cp:2 * cp + 2, :].rearrange("p c g -> p (c g)"), ident[:, :])
                return mm

            def pair(q, i):
                if i == 0:
                    misc_drained(q, PAIR)
                pair_into(misc_bank(q, PAIR + i), i).then_inc(misc_full, 1)

            def pair_into(ps, i):
                if i == 0:
                    for s in range(SPG):
                        mm = nc.tensor.transpose(ps[:, s * 128:(s + 1) * 128], pairs[:, s, 0:128], ident[:, :])
                else:
                    for s in reversed(range(SPG)):
                        nc.tensor.transpose(ps[0:FK[2], s * GPH:(s + 2) * GPH], pairs[:, s, 64:MERGED], ident[:, :])
                    for s in range(SPG):
                        mm = nc.tensor.transpose(ps[0:64, (s + 1) * GPH:(s + 3) * GPH], pairs[:, s, 128:POS], ident[:, :])
                return mm

            def product(out, terms, start=True, stop=True):
                for n, (w, x) in enumerate(terms):
                    mm = nc.tensor.matmul(out, w, x, start=start and n == 0, stop=stop and n == len(terms) - 1)
                return mm

            def three(w_hi, w_lo, x_hi, x_lo):
                return [(w_hi, x_hi), (w_lo, x_hi), (w_hi, x_lo)]

            def terms1(m, f):
                cols = slice(m * 128, (m + 1) * 128)
                if f == 0:
                    return three(w1d_hi[:, cols], w1d_lo[:, cols], dense_hi[:, :], dense_lo[:, :])
                f, n = f - 1, FK[f - 1]
                cols = slice(f * H1 + m * 128, f * H1 + (m + 1) * 128)
                return three(w1p_hi[0:n, cols], w1p_lo[0:n, cols], pairs_hi[0:n, f, :], pairs_lo[0:n, f, :])

            def terms2(m, c):
                cols, x = slice(c * H2 + m * 128, c * H2 + (m + 1) * 128), slice(c * HALF, (c + 1) * HALF)
                return three(w2_hi[:, cols], w2_lo[:, cols], h1_hi[:, x], h1_lo[:, x])

            def layer1(q, i):
                if i == 0:
                    misc_drained(q, LAYER1)
                    pe.wait_ge(split_lo, NJ)
                    pe.wait_ge(dense_split, q + 1)
                ps = misc_bank(q, LAYER1 + i)
                for m in (2 * i, 2 * i + 1):
                    mm = product(ps[:, m % 2 * HALF:(m % 2 + 1) * HALF],
                                 [term for f in range(FCH + 1) for term in terms1(m, f)])
                mm.then_inc(misc_full, 1)

            def layer2(q, m, first, last):
                if m == 0:
                    pe.wait_ge(h1_ready, M1 * (q + 1))
                    misc_bank(q, LAYER2)
                mm = product(misc_ps[LAYER2 % 2][:, m * HALF:(m + 1) * HALF],
                             [term for c in range(first, last) for term in terms2(m, c)],
                             start=(first == 0), stop=(last == M1))
                if m == M2 - 1 and last == M1:
                    mm.then_inc(misc_full, 1)

            def layer3(q):
                misc_drained(q, LAYER3)
                final(misc_bank(q, LAYER3)).then_inc(misc_full, 1)

            def final(ps):
                for a in range(2):
                    for c in range(M2):
                        mm = nc.tensor.matmul(ps[:, a:a + 1], h2[:, c, a * 128:(a + 1) * 128], w3s[:, c:c + 1],
                                              start=(c == 0), stop=(c == M2 - 1))
                return mm

            def half(k, first):
                q = None if first else k - 1
                for n in range(4):
                    hot(k, n, first)
                    if not first:
                        back(q, n)
                turn(k, 0, 0, 2, first)
                hot(k, 4, first)
                turn(k, 0, 2, 4, first)
                if not first:
                    pair(q, 0)
                hot(k, 5, first)
                turn(k, 0, 4, GR, first)
                if not first:
                    pair(q, 1)
                if NH > 6:
                    hot(k, 6, first)
                if first:
                    early()
                if not first:
                    layer1(q, 0)
                if NH > 7:
                    hot(k, 7, first)
                if not first:
                    layer1(q, 1)
                gram(k, 0)
                turn(k, 1, 0, 2, first)
                if not first:
                    layer2(q, 0, 0, M1)
                turn(k, 1, 2, 4, first)
                if not first:
                    layer2(q, 1, 0, 2)
                turn(k, 1, 4, GR, first)
                if not first:
                    layer2(q, 1, 2, M1)
                gram(k, 1)
                if not first:
                    layer3(q)

            pe.wait_ge(s_ident, 2)
            half(0, True)
            pe.wait_ge(s_consts, 48)
            with pe.Fori(1, NHALF) as k:
                half(k, False)

            pe.wait_ge(dots_v, 2 * GB * NHALF + 2)
            pe.wait_ge(dots_a, 2 * GB * NHALF + 2)
            misc_drained(NHALF - 1, 0)
            for i, ps in enumerate(END_BACK):
                back_into(ps, i).then_inc(end_full, 1)
            pe.wait_ge(dense_split, NHALF)
            for m in range(M1):
                product(END_LAYER1[m], terms1(m, 0), stop=False)
            pe.wait_ge(end_v, 2)
            pe.wait_ge(end_a, 2)
            for i, ps in enumerate(END_PAIR):
                pair_into(ps, i).then_inc(end_full, 1)
            pe.wait_ge(end_hi, 1)
            for m in range(M1):
                product(END_LAYER1[m], terms1(m, 1)[:2] + terms1(m, 2)[:2], start=False, stop=False)
            pe.wait_ge(end_lo, 2)
            for m in range(M1):
                product(END_LAYER1[m], terms1(m, 3) + terms1(m, 1)[2:] + terms1(m, 2)[2:], start=False)\
                    .then_inc(end_full, 1)
            for c in range(M1):
                for part in range(2):
                    pe.wait_ge((end_hi, end_lo)[part], 2 + c + 1)
                    for m in range(M2):
                        terms = terms2(m, c)[2:] if part else terms2(m, c)[:2]
                        mm = product(END_LAYER2[m], terms, start=(c == 0 and not part), stop=(c == M1 - 1 and part == 1))
                        if c == M1 - 1 and part:
                            mm.then_inc(end_full, 1)
            pe.wait_ge(end_v, END_H2)
            pe.wait_ge(end_a, END_H2)
            final(END_LAYER3).then_inc(end_full, 1)

        def turn_copy(eng, copy, k, t, g, is_first=False):
            u, group = t * GR + g, TGROUPS[g]
            eng.wait_ge(turn_full, 2 * GR * k + u + 1)
            w = len(group) - (1 if is_first and g == GR - 1 else 0)
            v = turn_ps[u % 2][:, 0:w * 128].rearrange("d (f s j) -> d j s f", f=w, s=SPG)
            copy(rows(t, 1 + group[0], w), v).then_inc(turned_v if TURNS[u] == "v" else turned_a, 1)

        def misc_wait(eng, q, i):
            eng.wait_ge(misc_full, USES * q + i + 1)

        def back_out(eng, copy, q, i):
            misc_wait(eng, q, i)
            pairs_from(copy, misc_ps[i % 2], i).then_inc(misc_v if DRAINS[i] == "v" else misc_a, 1)

        def pairs_from(copy, ps, i):
            cps = range(4 * i, min(4 * i + 4, CPAIRS))
            for m, cp in enumerate(cps):
                v = ps[:, m * 128:(m + 1) * 128].rearrange("g (s r) -> g s r", s=SPG)
                at = first_merged(cp)
                copy(pairs[:, :, at:at + width(cp)], v[:, :, 2 * cp + 2:2 * cp + 2 + width(cp)])
            v = ps[0:GPH, 8 * i + 1:8 * i + 2]
            at = MERGED + 4 * i
            v = bass.AP(v.tensor, v.offset, [v.ap[0], [ROWS, SPG], [128 + 2, len(cps)]])
            return copy(pairs[0:GPH, :, at:at + len(cps)], v)

        def pair_bank(i, ps=None):
            ps = ps or misc_ps[(PAIR + i) % 2]
            if i == 0:
                return (ps[:, :].rearrange("p (s f g) -> p f s g", s=SPG, f=2),
                        *(x[:, 0:2, :].rearrange("p f (s g) -> p f s g", s=SPG) for x in (pairs_hi, pairs_lo)))
            return ps[0:FK[2], GPH:GPH + HALF], pairs_hi[0:FK[2], 2, :], pairs_lo[0:FK[2], 2, :]

        @block.scalar
        def _(act):
            def copy(out, in_):
                return nc.scalar.activation(out, in_, ACT.Copy)

            def split(j):
                data = staged(act, j)
                copy(jobs[j][3], data).then_inc(split_hi, 1)

            def hot_out(k, b):
                w = min(2, NH - 2 * b)
                act.wait_ge(hot_done, NH * k + 2 * b + w)
                for t in range(2):
                    v = hot_ps[b % 2][:, 0:w * HALF].rearrange("d (f t j s) -> d t j s f", f=w, t=2, j=JT)
                    out = copy(rows(t, 1 + NG + 2 * b, w), v[:, t])
                out.then_inc(hot_in, 1)

            def early_out():
                act.wait_ge(early_done, 1)
                b, at = NH // 2, HALF * (NH % 2)
                for t in range(2):
                    v = hot_ps[b % 2][:, at:at + HALF].rearrange("d (f t j s) -> d t j s f", f=1, t=2, j=JT)
                    copy(rows(t, NG, 1), v[:, t])

            def turn_out(k, t, first, last, is_first=False):
                for g in range(first, last):
                    if TURNS[t * GR + g] == "a":
                        turn_copy(act, copy, k, t, g, is_first)

            def dots_out(k, t, between={}):
                for b in range(GB):
                    if b in between:
                        between[b]()
                    act.wait_ge(dots_full, 2 * GB * k + t * GB + b + 1)
                    for s in (2, 3):
                        out = copy(dots_part(t, b, s), dots_bank(b, s))
                    out.then_inc(dots_a, 1)

            def pair_hi(q, i):
                misc_wait(act, q, PAIR + i)
                ps, high, low = pair_bank(i)
                copy(high, ps).then_inc(pairs_hi_ready, 1)

            def layer1_out(q, i):
                misc_wait(act, q, LAYER1 + i)
                for m in (2 * i, 2 * i + 1):
                    out = nc.scalar.activation(h1[:, m * HALF:(m + 1) * HALF],
                                               misc_ps[(LAYER1 + i) % 2][:, m % 2 * HALF:(m % 2 + 1) * HALF],
                                               ACT.Relu, bias=b1s[:, m:m + 1])
                out.then_inc(misc_a, 1)

            def layer1_hi(q, i):
                act.wait_ge(misc_a, DRAINS.count("a") * q + drained_before(LAYER1 + i + 1)[1] + 1)
                part = slice(2 * i * HALF, (2 * i + 2) * HALF)
                copy(h1_hi[:, part], h1[:, part]).then_inc(h1_hi_ready, 1)

            def layer2_out(q):
                misc_wait(act, q, LAYER2)
                for m in range(M2):
                    out = nc.scalar.activation(h2[:, m, :], misc_ps[LAYER2 % 2][:, m * HALF:(m + 1) * HALF],
                                               ACT.Relu, bias=b2s[:, m:m + 1])
                out.then_inc(misc_a, 1)

            def dense_hi_out(k):
                act.wait_ge(s_dense, 16 * (k + 1))
                copy(dense_hi[:, :], dense[:, :]).then_inc(dense_split_hi, 1)

            def half(k, first):
                q = None if first else k - 1
                for n in range(4):
                    if n % 2:
                        hot_out(k, n // 2)
                    if not first:
                        back_out(act, copy, q, n)
                turn_out(k, 0, 0, 4)
                if not first:
                    pair_hi(q, 0)
                turn_out(k, 0, 4, GR, first)
                hot_out(k, 2)
                if not first:
                    pair_hi(q, 1)
                if first and NH % 2:
                    early_out()
                if NH == 7:
                    hot_out(k, 3)
                if not first:
                    layer1_out(q, 0)
                    layer1_hi(q, 0)
                if NH == 8:
                    hot_out(k, 3)
                if not first:
                    layer1_out(q, 1)
                if first:
                    act.wait_ge(split_lo, TJ)
                dots_out(k, 0, {1: lambda: first or layer1_hi(q, 1), 4: lambda: dense_hi_out(k)})
                if first:
                    for j in range(TJ, NJ):
                        split(j)
                turn_out(k, 1, 0, GR, first)
                if not first:
                    layer2_out(q)
                dots_out(k, 1)

            for j in range(TJ):
                split(j)
            act.wait_ge(s_consts, 48)
            half(0, True)
            with act.Fori(1, NHALF) as k:
                half(k, False)

            def h1_hi_end(m):
                part = slice(m * HALF, (m + 1) * HALF)
                act.wait_ge((end_a, end_v)[m % 2], END_H1 + m // 2 + 1)
                copy(h1_hi[:, part], h1[:, part]).then_inc(end_hi, 1)

            for i in (0, 2):
                act.wait_ge(end_full, i + 1)
                pairs_from(copy, END_BACK[i], i).then_inc(end_a, 1)
            for i in range(2):
                act.wait_ge(end_full, 4 + i + 1)
                ps, high, low = pair_bank(i, END_PAIR[i])
                copy(high, ps).then_inc(end_hi, 1)
            for m in (0, 2):
                act.wait_ge(end_full, 6 + m + 1)
                nc.scalar.activation(h1[:, m * HALF:(m + 1) * HALF], END_LAYER1[m], ACT.Relu, bias=b1s[:, m:m + 1])\
                  .then_inc(end_a, 1)
                h1_hi_end(m)
                h1_hi_end(m + 1)
            act.wait_ge(end_full, 11)
            nc.scalar.activation(h2[:, 0, :], END_LAYER2[0], ACT.Relu, bias=b2s[:, 0:1]).then_inc(end_a, 1)

        @block.vector
        def _(dve):
            def copy(out, in_):
                return nc.vector.tensor_copy(out, in_)

            def rest(out, full, high):
                return nc.vector.tensor_tensor(out, full, high, ALU.subtract)

            def split(j):
                data = staged(dve, j)
                dve.wait_ge(split_hi, j + 1)
                rest(jobs[j][4], data, jobs[j][3]).then_inc(split_lo, 1)

            def stage(t, tile):
                copy(index[:, t, :], ids_sb[:, bass.ds(tile, 1), :].rearrange("p a f -> p (a f)"))\
                    .then_inc(index_ready[t], 1)

            def stage_next(k, t):
                dve.wait_ge(turn_full, 2 * GR * k + GR * (t + 1))
                stage(t, 2 * k + t + 2)

            def one_hot(n, chunks=range(HOT_CH)):
                ids = ids_cast[0:HOT_K, n * HALF:(n + 1) * HALF]
                for c in chunks:
                    out = nc.vector.tensor_scalar(onehot[0:HOT_K, n % UNITS, c, :], ids, row_id[0:HOT_K, c:c + 1], None,
                                                  ALU.is_equal)
                if c == HOT_CH - 1:
                    out.then_inc(onehot_ready, 1)

            def one_hot_early():
                dve.wait_ge(s_cast_early, 16)
                dve.wait_ge(hot_done, NH - UNITS + 1)
                for c in range(HOT_CH):
                    out = nc.vector.tensor_scalar(onehot[0:HOT_K, NH % UNITS, c, :], ids_cast_early[0:HOT_K, :],
                                                  row_id[0:HOT_K, c:c + 1], None, ALU.is_equal)
                out.then_inc(early_ready, 1)

            def one_hot_again(k, n):
                dve.wait_ge(hot_done, NH * k + n - UNITS + 1)
                one_hot(n)

            def dense_rows(k):
                dve.wait_ge(s_dense, 16 * (k + 1))
                for t in range(2):
                    v = dense[:, :].rearrange("d (s t j) -> d t j s", s=SPG, t=2)
                    out = copy(rows(t, 0, 1).rearrange("d j s r -> d j (s r)"), v[:, t])
                out.then_inc(dense_in, 1)

            def dots_out(k, t, between={}, ahead={}):
                for b in range(GB):
                    if b in between:
                        between[b]()
                    dve.wait_ge(dots_full, 2 * GB * k + t * GB + b + 1)
                    for s in (0, 1):
                        out = copy(dots_part(t, b, s), dots_bank(b, s))
                    out.then_inc(dots_v, 1)
                    if b in ahead:
                        one_hot_ahead(*ahead[b])

            def one_hot_ahead(first, count):
                for i in range(first, first + count):
                    one_hot(i // HOT_CH, [i % HOT_CH])

            def pair_lo(q, i):
                dve.wait_ge(pairs_hi_ready, 2 * q + i + 1)
                ps, high, low = pair_bank(i)
                rest(low, ps, high).then_inc(misc_v, 1)

            def h1_lo_out(q, i):
                dve.wait_ge(h1_hi_ready, 2 * q + i // 2 + 1)
                part = slice(i * HALF, (i + 1) * HALF)
                rest(h1_lo[:, part], h1[:, part], h1_hi[:, part]).then_inc(h1_ready, 1)

            def dense_lo_out(k):
                dve.wait_ge(dense_split_hi, k + 1)
                rest(dense_lo[:, :], dense[:, :], dense_hi[:, :]).then_inc(dense_split, 1)

            def result(q):
                misc_wait(dve, q, LAYER3)
                copy(ys[:, bass.ds(2 * q, 2)], misc_ps[LAYER3 % 2][:, 0:2]).then_inc(misc_v, 1)

            def half(k, first):
                q = None if first else k - 1
                dense_rows(k)
                for n in range(UNITS, NH):
                    if first:
                        split(n)
                    one_hot_again(k, n)
                if first:
                    split(NH)
                    one_hot_early()
                if not first:
                    pair_lo(q, 0)
                stage_next(k, 0)
                if not first:
                    pair_lo(q, 1)
                    for i in range(2):
                        h1_lo_out(q, i)
                dve.wait_ge(s_cast[0], 16 * (k + 2))
                dve.wait_ge(hot_done, NH * (k + 1))
                if first:
                    dve.wait_ge(early_done, 1)
                dots_out(k, 0, {} if first else {2: lambda: h1_lo_out(q, 2), 3: lambda: h1_lo_out(q, 3)},
                         {b: (b - 4, 1) for b in range(4, GB)})
                if first:
                    for j in range(TJ, NJ):
                        if j == FOLD:
                            dve.wait_ge(s_raw[jobs[j][0]], 16 * sum(job[0] == jobs[j][0] for job in jobs))
                            v = raw[jobs[j][0]]
                            nc.vector.tensor_tensor(v[:, 0:H1], v[:, 0:H1], v[:, H1:2 * H1], ALU.add).then_inc(s_fold, 1)
                        split(j)
                    dve.wait_ge(split_lo, NJ)
                    nc.vector.memset(pairs[:, :, MERGED + CPAIRS:POS], 0.0)
                for g in range(GR):
                    if TURNS[GR + g] == "v":
                        turn_copy(dve, copy, k, 1, g)
                        if g == 1:
                            one_hot_ahead(4, 4)
                            dense_lo_out(k)
                stage_next(k, 1)
                dots_out(k, 1, {}, {b: (8 + 2 * b, 2) for b in range(GB)})
                if not first:
                    result(q)

            nc.vector.memset(rows(0, SLOTS, ROWS - SLOTS), 0.0).then_inc(hot_in, 1)
            nc.vector.memset(rows(1, SLOTS, ROWS - SLOTS), 0.0).then_inc(hot_in, 1)
            nc.vector.memset(ids_sb[:, 2 * NHALF:, :], 0).then_inc(dots_v, 2)
            nc.vector.memset(scrap[:, 0:1], 0.0).then_inc(dots_a, 2)
            nc.vector.memset(scrap[:, 1:2], 0.0).then_inc(misc_v, 1)
            nc.vector.memset(scrap[:, 2:3], 0.0).then_inc(misc_a, 1)
            dve.wait_ge(s_ids, 16)
            for t in range(2):
                stage(t, t)
            dve.wait_ge(s_rowid, 1)
            copy(row_id[:, :], row_id_i[:, :]).then_inc(s_rowid_f, 1)
            dve.wait_ge(s_rowid_f, 1)
            dve.wait_ge(s_cast[0], 16)
            for n in range(UNITS):
                one_hot(n)
                split(n)
            dve.wait_ge(s_cast[1], 16)
            half(0, True)
            with dve.Fori(1, NHALF) as k:
                dve.wait_ge(s_cast[1], 16 * (k + 1))
                half(k, False)

            def h1_lo_end(m):
                part = slice(m * HALF, (m + 1) * HALF)
                dve.wait_ge(end_hi, 2 + m + 1)
                rest(h1_lo[:, part], h1[:, part], h1_hi[:, part]).then_inc(end_lo, 1)

            def relu(out, ps, bias):
                return nc.vector.tensor_scalar(out, ps, bias, 0.0, ALU.add, ALU.max)

            for i in (1, 3):
                dve.wait_ge(end_full, i + 1)
                pairs_from(copy, END_BACK[i], i).then_inc(end_v, 1)
            for i in range(2):
                dve.wait_ge(end_hi, i + 1)
                ps, high, low = pair_bank(i, END_PAIR[i])
                rest(low, ps, high).then_inc(end_lo, 1)
            for m in (1, 3):
                dve.wait_ge(end_full, 6 + m + 1)
                relu(h1[:, m * HALF:(m + 1) * HALF], END_LAYER1[m], b1s[:, m:m + 1]).then_inc(end_v, 1)
                h1_lo_end(m - 1)
                h1_lo_end(m)
            dve.wait_ge(end_full, 12)
            relu(h2[:, 1, :], END_LAYER2[1], b2s[:, 1:2]).then_inc(end_v, 1)
            dve.wait_ge(end_full, 13)
            copy(ys[:, 2 * (NHALF - 1):], END_LAYER3[:, 0:2]).then_inc(end_v, 1)


def kernel(**inputs):
    import numpy as _np
    import concourse.bacc as _bacc
    from concourse import mybir as _mybir
    from concourse.bass_utils import run_bass_kernel_spmd as _run

    a = {name: _np.asarray(v) for name, v in inputs.items()}
    w1 = a["W_top1"]

    def weight_rows(found):
        rows = []
        for c, r in found:
            if c == 0:
                rows.append(D + ORDER[r - 1])
            else:
                f, g = sorted((ORDER[c - 1], ORDER[r - 1]))
                rows.append(D + TABLES + f * (TABLES - 1) - f * (f - 1) // 2 + g - f - 1)
        return w1[rows]

    even, odd = ([(c + side, r) for c in range(0, COLS, 2) for r in range(c + 2, SLOTS)] for side in (0, 1))
    even += [(c, c + 1) for c in range(0, COLS, 2)]
    w1_pairs = [weight_rows(even[:128]), weight_rows(odd[:128]), weight_rows(even[128:]),
                _np.zeros((POS - len(even), H1), w1.dtype), weight_rows(odd[128:])]
    ids = a["ids"].reshape(NHALF // 2, SPG, 2, 2, JT, TABLES)
    ids_tiles = ids.transpose(1, 4, 0, 2, 3, 5).reshape(TILE, 2 * NHALF, TABLES)
    ids_hot = ids[..., HOT].transpose(0, 2, 5, 3, 4, 1).reshape(NHALF, NH * HALF)
    dense = a["r_dense_features"].reshape(NHALF // 2, SPG, 2, GPH, D).transpose(0, 2, 4, 1, 3).reshape(NHALF, D, HALF)
    arrays = {
        "ids_tiles": ids_tiles,
        "ids_hot": _np.concatenate([ids_hot, ids_hot[:2]]),
        "ids_early": _np.ascontiguousarray(ids[0, :, 0, :, :, EARLY].transpose(1, 2, 0)).reshape(HALF),
        "dense_t": _np.concatenate([dense, dense[:1]]),
        "w1_dense": _np.concatenate([w1[:D], w1[-D:]]),
        "w1_pairs": _np.concatenate(w1_pairs),
        "b1": a["b_top1"].reshape(-1, 128).T,
        "w2": a["W_top2"],
        "b2": a["b_top2"].reshape(-1, 128).T,
        "w3": a["W_top3"].reshape(-1, 128).T,
    }
    arrays.update({f"tbl_{t}": a[f"tbl_{t}"] for t in range(TABLES)})
    nc = _bacc.Bacc("TRN2", target_bir_lowering=False, num_devices=1)
    h = {}
    for name in arrays:
        arrays[name] = _np.ascontiguousarray(arrays[name])
        h[name] = nc.dram_tensor(name, arrays[name].shape, _mybir.dt.from_np(arrays[name].dtype), kind="ExternalInput").ap()
    y = nc.dram_tensor("y", (128, NHALF * 2), _mybir.dt.float32, kind="ExternalOutput").ap()
    build(nc, h["ids_tiles"], h["ids_hot"], h["ids_early"], h["dense_t"], [h[f"tbl_{t}"] for t in range(TABLES)], h["w1_dense"],
          h["w1_pairs"], h["b1"], h["w2"], h["b2"], h["w3"], y)
    r = _run(nc, [arrays], core_ids=[0])
    out = r.results[0]["y"].reshape(2, GPH, NHALF // 2, 2, 2)
    return _np.ascontiguousarray(out.transpose(2, 4, 0, 3, 1)).reshape(BATCH, 1)
```

```python
from contextlib import ExitStack

import concourse.bass as bass
from concourse import mybir

BATCH, TABLES, D = 2048, 26, 128
HALF, TILE, SPG = 256, 128, 4
JT = TILE // SPG
GPH = HALF // SPG
NHALF = BATCH // HALF
SLOTS = TABLES + 1
COLS = TABLES
ROWS = 32
CPAIRS = COLS // 2
MERGED = sum(TABLES - 1 - c for c in range(0, COLS, 2))
REST = MERGED - 128
POS = 128 + 64
FCH = 3
FK = [128, 128, 64 + REST]
H1, H2 = 512, 256
M1, M2 = H1 // 128, H2 // 128
HOT_ROWS = 1000
HOT_CH = 8
HOT_K = HOT_ROWS // HOT_CH
HOT = [6, 8, 10, 11, 17, 19]
EXTRA = [25, 21]
MORE = 4
GATHERED = [t for t in range(TABLES) if t not in HOT + EXTRA] + EXTRA[::-1]
ORDER = GATHERED + HOT
NG, NH, NE = len(GATHERED), len(HOT), len(EXTRA)
TGROUPS = [list(range(a, min(a + 4, NG))) for a in range(0, NG, 4)]
GR = len(TGROUPS)
GB = JT // 4
UNITS = 3
HB = (NH + 1) // 2
TURNS = "a" * GR + "avavavav"[:GR]
RAW = 3

BACK, PAIR, LAYER1, LAYER2, LAYER3, USES = 0, 4, 6, 8, 9, 10
DRAINS = "aaaa" "vv" "aa" "a" "v"


def drained_before(i):
    return DRAINS[:i].count("v"), DRAINS[:i].count("a")


def turned_before(u):
    return TURNS[:u].count("v"), TURNS[:u].count("a")


def width(cp):
    return TABLES - 1 - 2 * cp


def first_merged(cp):
    return sum(width(i) for i in range(cp))


def extras(kind):
    return {"first": NE, "more": 1, "rest": 0}[kind]


def extras_through(kind, k):
    return {"first": NE, "more": NE + k, "rest": NE + MORE - 1}[kind]


def gathered_through(kind, k):
    return {"first": NG - NE, "more": (NG - 1) * k + NG - NE, "rest": NG * k + NG - extras_through("rest", 0)}[kind]


def build(nc, ids_tiles, ids_hot, ids_extra, dense_t, tables, w1_dense, w1_pairs, b1, w2, b2, w3, y):
    fp32, f32r, i32 = mybir.dt.float32, mybir.dt.float32r, mybir.dt.int32
    ALU, ACT = mybir.AluOpType, mybir.ActivationFunctionType

    ctx = ExitStack()
    with ctx:
        def sb(name, shape, dt=fp32):
            return ctx.enter_context(nc.sbuf_tensor(name, shape, dt))

        def sem(name):
            return ctx.enter_context(nc.semaphore(name))

        ids_sb = sb("ids_sb", [128, 2 * NHALF + 2, TABLES], i32)
        index = sb("index", [128, 2, TABLES], i32)
        ids_cast = sb("ids_cast", [128, NH * HALF], i32)
        ids_cast_extra = sb("ids_cast_extra", [128, NE, HALF], i32)
        dense = sb("dense", [D, HALF])
        dense_hi, dense_lo = sb("dense_hi", [D, HALF], f32r), sb("dense_lo", [D, HALF], f32r)
        emb = sb("emb", [128, 2, NG * D])
        embT = sb("embT", [D, 2, JT, SPG, ROWS])
        onehot = sb("onehot", [128, UNITS, HOT_CH, HALF], f32r)
        hot_hi = sb("hot_hi", [HOT_K, NH, HOT_CH * D], f32r)
        hot_lo = sb("hot_lo", [HOT_K, NH, HOT_CH * D], f32r)
        row_id = sb("row_id", [128, HOT_CH])
        row_id_i = sb("row_id_i", [128, HOT_CH], i32)
        dots = sb("dots", [128, COLS, GPH])
        pairs_all = sb("pairs_all", [128, HOT_CH * D])
        pairs = pairs_all[:, 0:SPG * POS].rearrange("p (s f) -> p s f", s=SPG)
        pairs_hi, pairs_lo = sb("pairs_hi", [128, FCH, HALF], f32r), sb("pairs_lo", [128, FCH, HALF], f32r)
        w1d_hi, w1d_lo = sb("w1d_hi", [128, H1], f32r), sb("w1d_lo", [128, H1], f32r)
        w1p_hi, w1p_lo = sb("w1p_hi", [128, FCH * H1], f32r), sb("w1p_lo", [128, FCH * H1], f32r)
        w2_hi, w2_lo = sb("w2_hi", [128, M1 * H2], f32r), sb("w2_lo", [128, M1 * H2], f32r)
        w3s = sb("w3s", [128, M2])
        b1s = sb("b1s", [128, M1])
        b2s = sb("b2s", [128, M2])
        h1 = sb("h1", [128, M1 * HALF])
        h1_hi, h1_lo = sb("h1_hi", [128, M1 * HALF], f32r), sb("h1_lo", [128, M1 * HALF], f32r)
        h2 = sb("h2", [128, M2, HALF])
        ys = sb("ys", [128, NHALF * 2])
        ident = sb("ident", [128, 128])
        extra_hi = [sb("extra_hi", [HOT_K, HOT_CH * D], f32r), h1_hi]
        extra_lo = [sb("extra_lo", [HOT_K, HOT_CH * D], f32r), h1_lo]
        scrap = sb("scrap", [1, 4])
        raw = [dots[:, :, :].rearrange("p c g -> p (c g)"), pairs_all, h1]

        def bank(name):
            return ctx.enter_context(nc.psum_tensor(name, [128, 512], fp32))

        turn_ps = [bank(f"turn_ps{i}") for i in range(2)]
        hot_ps = [bank(f"hot_ps{i}") for i in range(2)]
        dots_ps = [bank(f"dots_ps{i}") for i in range(2)]
        misc_ps = [bank(f"misc_ps{i}") for i in range(2)]

        s_ids, s_out = sem("s_ids"), sem("s_out")
        s_cast_first = sem("s_cast_first")
        s_index = sem("s_index")
        s_consts = sem("s_consts")
        s_dense = sem("s_dense")
        s_cast = [sem(f"s_cast{i}") for i in range(2)]
        s_raw = [sem(f"s_raw{i}") for i in range(RAW)]
        s_fold = sem("s_fold")
        s_ident, s_rowid, s_rowid_f = sem("s_ident"), sem("s_rowid"), sem("s_rowid_f")
        split_hi, split_lo = sem("split_hi"), sem("split_lo")
        index_ready = [sem(f"index_ready{t}") for t in range(2)]
        gathered = [sem(f"gathered{t}") for t in range(2)]
        turn_full = sem("turn_full")
        turned_v, turned_a = sem("turned_v"), sem("turned_a")
        dense_in = sem("dense_in")
        dense_split_hi, dense_split = sem("dense_split_hi"), sem("dense_split")
        onehot_ready, hot_done = sem("onehot_ready"), sem("hot_done")
        s_cast_extra = [sem(f"s_cast_extra{e}") for e in range(NE)]
        extra_ready, extra_done, extra_in = sem("extra_ready"), sem("extra_done"), sem("extra_in")
        hot_in = sem("hot_in")
        dots_full = sem("dots_full")
        dots_v, dots_a = sem("dots_v"), sem("dots_a")
        misc_full = sem("misc_full")
        misc_v, misc_a = sem("misc_v"), sem("misc_a")
        pairs_hi_ready = sem("pairs_hi_ready")
        h1_hi_ready, h1_ready = sem("h1_hi_ready"), sem("h1_ready")

        end_full, end_v, end_a, end_hi, end_lo = (sem(f"end_{x}") for x in ("full", "v", "a", "hi", "lo"))
        END_BACK = misc_ps + turn_ps
        END_PAIR, END_LAYER1 = misc_ps, [ps[:, 0:HALF] for ps in hot_ps + dots_ps]
        END_LAYER2, END_LAYER3 = [ps[:, 0:HALF] for ps in turn_ps], misc_ps[0]
        END_H1, END_H2, END_Y = 2, 5, 6

        block = ctx.enter_context(nc.Block())

        def rows(slot, first, count):
            return embT[:, slot, :, :, first:first + count]

        def dots_part(t, b, s):
            at = t * JT + 4 * b
            return dots[32 * s:32 * s + 32, :, at:at + 4]

        def dots_bank(b, s):
            v = dots_ps[b % 2][32 * s:32 * s + 32, :].rearrange("p (g c) -> p c g", g=4)
            return v[:, s * 32:s * 32 + COLS, :]

        def turned_tables(g, kind):
            return [n for n in TGROUPS[g] if n < NG - extras(kind)]

        jobs = [(n % RAW, HOT_K, HOT_CH * D, hot_hi[:, n, :], hot_lo[:, n, :]) for n in range(NH)]
        jobs += [((NH + e) % RAW, HOT_K, HOT_CH * D, extra_hi[e][0:HOT_K, :], extra_lo[e][0:HOT_K, :]) for e in range(NE)]
        jobs.append((2, 128, M1 * H2, w2_hi[:, :], w2_lo[:, :]))
        jobs.append((1, 128, 2 * H1, w1p_hi[:, 0:2 * H1], w1p_lo[:, 0:2 * H1]))
        jobs.append((2, FK[2], H1, w1p_hi[0:FK[2], 2 * H1:3 * H1], w1p_lo[0:FK[2], 2 * H1:3 * H1]))
        jobs.append((1, 128, H1, w1d_hi[:, :], w1d_lo[:, :]))
        TJ, NJ, FOLD = NH + NE, len(jobs), len(jobs) - 1

        def staged(eng, j):
            slot, parts, size = jobs[j][:3]
            eng.wait_ge(s_raw[slot], 16 * sum(job[0] == slot for job in jobs[:j + 1]))
            if j == FOLD:
                eng.wait_ge(s_fold, 1)
            return raw[slot][0:parts, 0:size]

        @block.sync
        def _(sp):
            def load_cast(part, half, first=0):
                a, b = (first * HALF, UNITS * HALF) if part == 0 else (UNITS * HALF, NH * HALF)
                src = ids_hot[bass.ds(half, 1), a:b]
                sp.dma_start(ids_cast[:, a:b], bass.AP(src.tensor, src.offset, [[0, 128], [1, b - a]]))\
                  .then_inc(s_cast[part], 16)

            def load_cast_extra(e, half):
                src = ids_extra[e:e + 1, bass.ds(half * HALF, HALF)]
                sp.dma_start(ids_cast_extra[:, e, :], bass.AP(src.tensor, src.offset, [[0, 128], [1, HALF]]))\
                  .then_inc(s_cast_extra[e], 16)

            def load_dense(half):
                sp.dma_start(dense[:, :], dense_t[bass.ds(half, 1), :, :].rearrange("a d n -> d (a n)"))\
                  .then_inc(s_dense, 16)

            sources = [tables[t].rearrange("(p c) d -> p (c d)", c=HOT_CH) for t in HOT + EXTRA]
            sources.append(w2.rearrange("(a p) n -> p a n", p=128))
            sources.append(w1_pairs[0:256, :].rearrange("(a p) n -> p a n", a=2))
            sources.append(w1_pairs[256:, :])
            sources.append(w1_dense.rearrange("(a p) n -> p a n", a=2))

            def load_job(j):
                slot, parts, size = jobs[j][:3]
                before = [i for i in range(j) if jobs[i][0] == slot]
                if before:
                    sp.wait_ge(split_lo, before[-1] + 1)
                if j == FOLD:
                    size = 2 * H1
                out = raw[slot][0:parts, 0:size]
                if len(sources[j].shape) == 3:
                    out = out.rearrange("p (a n) -> p a n", a=sources[j].shape[1])
                sp.dma_start(out, sources[j]).then_inc(s_raw[slot], 16)

            sp.dma_start(index[:, :, :], ids_tiles[:, 0:2, :]).then_inc(s_index, 16)
            sp.dma_start(ids_cast[:, 0:HALF], bass.AP(ids_hot.tensor, ids_hot.offset, [[0, 128], [1, HALF]]))\
              .then_inc(s_cast_first, 16)
            load_job(0)
            load_cast(0, 0, 1)
            load_job(1)
            load_cast(1, 0)
            load_job(2)
            load_dense(0)
            load_job(3)
            load_job(4)
            load_cast_extra(0, 0)
            load_job(5)
            load_cast_extra(1, 0)
            load_job(6)
            sp.dma_start(ids_sb[:, 0:2 * NHALF, :], ids_tiles).then_inc(s_ids, 16)
            load_job(7)
            sp.wait_ge(onehot_ready, UNITS)
            load_cast(0, 1)
            sp.dma_start(w3s[:, :], w3).then_inc(s_consts, 16)
            sp.dma_start(b1s[:, :], b1).then_inc(s_consts, 16)
            sp.dma_start(b2s[:, :], b2).then_inc(s_consts, 16)
            for j in range(TJ, NJ):
                load_job(j)

            def load_next(k):
                sp.wait_ge(onehot_ready, NH * (k + 1))
                load_cast(1, k + 1)
                sp.wait_ge(dense_split, k + 1)
                load_dense(k + 1)
                sp.wait_ge(onehot_ready, NH * (k + 1) + UNITS)
                load_cast(0, k + 2)

            with sp.Fori(0, MORE - 1) as k:
                sp.wait_ge(extra_ready, extras_through("more", k))
                load_cast_extra(0, k + 1)
                load_next(k)
            with sp.Fori(MORE - 1, NHALF) as k:
                load_next(k)
            sp.wait_ge(end_v, END_Y)
            sp.dma_start(y, ys[:, :]).then_inc(s_out, 16)
            sp.wait_ge(s_out, 16)
            sp.wait_ge(s_cast[0], 16 * (NHALF + 2))
            sp.wait_ge(s_cast[1], 16 * (NHALF + 1))
            sp.wait_ge(s_dense, 16 * (NHALF + 1))

        @block.gpsimd
        def _(pool):
            pool.iota(row_id_i[:, :], [[1, HOT_CH]], base=0, channel_multiplier=HOT_CH).then_inc(s_rowid, 1)
            pool.memset(ident[:, :], 0.0).then_inc(s_ident, 1)
            pool.wait_ge(s_ident, 1)
            pool.affine_select(out=ident[:, :], in_=ident[:, :], compare_op=ALU.not_equal, fill=1.0,
                               base=0, pattern=[[-1, 128]], channel_multiplier=1).then_inc(s_ident, 1)

            def gather(k, t, tables_of_half):
                if k is not None:
                    pool.wait_ge(index_ready[t], k)
                else:
                    pool.wait_ge(s_index, 16)
                pool.nop(nofuse=True)
                for n, table in enumerate(tables_of_half):
                    pool.indirect_dma_start(
                        emb[:, t, n * D:(n + 1) * D], None, tables[table],
                        bass.IndirectOffsetOnAxis(index[:, t, table:table + 1], 0)).then_inc(gathered[t], 16)

            for t in range(2):
                gather(None, t, GATHERED[:NG - NE])
            with pool.Fori(1, MORE) as k:
                for t in range(2):
                    gather(k, t, GATHERED[:NG - 1])
            with pool.Fori(MORE, NHALF) as k:
                for t in range(2):
                    gather(k, t, GATHERED)

        @block.tensor
        def _(pe):
            def hot(k, n, first):
                b = n // 2
                if n % 2 == 0:
                    pe.wait_ge(hot_in, HB * k + b + 1)
                if first:
                    pe.wait_ge(split_lo, n + 1)
                pe.wait_ge(onehot_ready, NH * k + n + 1)
                out = hot_ps[b % 2][:, (n % 2) * HALF:(n % 2 + 1) * HALF]
                look_up(out, hot_hi[:, n, :], hot_lo[:, n, :], n % UNITS).then_inc(hot_done, 1)

            def look_up(out, high, low, unit):
                for c in range(HOT_CH):
                    for part in (high, low):
                        mm = nc.tensor.matmul(out, part[:, c * D:(c + 1) * D], onehot[0:HOT_K, unit, c, :],
                                              start=(c == 0 and part is high),
                                              stop=(c == HOT_CH - 1 and part is low))
                return mm

            def extra(k, e, kind):
                n = NH + e
                if n % 2 == 0:
                    pe.wait_ge(hot_in, HB * k + n // 2 + 1)
                if kind == "first":
                    pe.wait_ge(split_lo, n + 1)
                pe.wait_ge(extra_ready, e + 1 if kind == "first" else extras_through(kind, k))
                look_up(hot_ps[n // 2 % 2][:, HALF * (n % 2):HALF * (n % 2 + 1)], extra_hi[e][0:HOT_K, :],
                        extra_lo[e][0:HOT_K, :], n % UNITS).then_inc(extra_done, 1)

            def turn_drained(k, u):
                done, engine = turned_before(u % (2 * GR) + 1), TURNS[u]
                at, count = ("va".index(engine), TURNS.count(engine))
                pe.wait_ge((turned_v, turned_a)[at], count * (k - 1 if u < 0 else k) + done[at])

            def turn(k, t, first, last, kind):
                if first == 0:
                    pe.wait_ge(gathered[t], 16 * gathered_through(kind, k))
                for g in range(first, last):
                    u = t * GR + g
                    if u >= 2 or kind != "first":
                        turn_drained(k, u - 2)
                    for m, n in enumerate(turned_tables(g, kind)):
                        mm = nc.tensor.transpose(turn_ps[u % 2][:, m * 128:(m + 1) * 128],
                                                 emb[:, t, n * D:(n + 1) * D], ident[:, :])
                    mm.then_inc(turn_full, 1)

            def gram(k, t):
                done = turned_before(GR * (t + 1))
                if t == 1:
                    pe.wait_ge(turned_v, TURNS.count("v") * k + done[0])
                pe.wait_ge(turned_a, TURNS.count("a") * k + done[1])
                pe.wait_ge(dense_in, k + 1)
                pe.wait_ge(hot_in, HB * (k + 1) + 2)
                for b in range(GB):
                    u = t * GB + b
                    pe.wait_ge(dots_v, 2 * GB * k + u + 1)
                    pe.wait_ge(dots_a, 2 * GB * k + u + 1)
                    for m in range(4):
                        group = embT[:, t, 4 * b + m, :, :]
                        out = dots_ps[b % 2][:, m * 128:(m + 1) * 128].rearrange("p (s c) -> p s c", s=SPG)
                        mm = nc.tensor.matmul(out[:, :, 0:COLS], group.rearrange("d s r -> d (s r)"),
                                              group[:, :, 0:COLS], start=True, stop=True)
                    mm.then_inc(dots_full, 1)

            def misc_bank(q, i):
                before = (i - 2) % USES
                done = drained_before(before + 1)
                at = 1 if DRAINS[before] == "a" else 0
                n = DRAINS.count(DRAINS[before])
                pe.wait_ge((misc_v, misc_a)[at], n * q + (1 if i < 2 else done[at] + 1))
                return misc_ps[i % 2]

            def misc_drained(q, i):
                done = drained_before(i)
                pe.wait_ge(misc_v, DRAINS.count("v") * q + done[0] + 1)
                pe.wait_ge(misc_a, DRAINS.count("a") * q + done[1] + 1)

            def back(q, i):
                if i == 0:
                    pe.wait_ge(dots_v, 2 * GB * (q + 1) + 2)
                    pe.wait_ge(dots_a, 2 * GB * (q + 1) + 2)
                back_into(misc_bank(q, BACK + i), i).then_inc(misc_full, 1)

            def back_into(ps, i):
                for m, cp in enumerate(range(4 * i, min(4 * i + 4, CPAIRS))):
                    mm = nc.tensor.transpose(ps[:, m * 128:(m + 1) * 128],
                                             dots[:, 2 * cp:2 * cp + 2, :].rearrange("p c g -> p (c g)"), ident[:, :])
                return mm

            def pair(q, i):
                if i == 0:
                    misc_drained(q, PAIR)
                pair_into(misc_bank(q, PAIR + i), i).then_inc(misc_full, 1)

            def pair_into(ps, i):
                if i == 0:
                    for s in range(SPG):
                        mm = nc.tensor.transpose(ps[:, s * 128:(s + 1) * 128], pairs[:, s, 0:128], ident[:, :])
                else:
                    for s in reversed(range(SPG)):
                        nc.tensor.transpose(ps[0:FK[2], s * GPH:(s + 2) * GPH], pairs[:, s, 64:MERGED], ident[:, :])
                    for s in range(SPG):
                        mm = nc.tensor.transpose(ps[0:64, (s + 1) * GPH:(s + 3) * GPH], pairs[:, s, 128:POS], ident[:, :])
                return mm

            def product(out, terms, start=True, stop=True):
                for n, (w, x) in enumerate(terms):
                    mm = nc.tensor.matmul(out, w, x, start=start and n == 0, stop=stop and n == len(terms) - 1)
                return mm

            def three(w_hi, w_lo, x_hi, x_lo):
                return [(w_hi, x_hi), (w_lo, x_hi), (w_hi, x_lo)]

            def terms1(m, f):
                cols = slice(m * 128, (m + 1) * 128)
                if f == 0:
                    return three(w1d_hi[:, cols], w1d_lo[:, cols], dense_hi[:, :], dense_lo[:, :])
                f, n = f - 1, FK[f - 1]
                cols = slice(f * H1 + m * 128, f * H1 + (m + 1) * 128)
                return three(w1p_hi[0:n, cols], w1p_lo[0:n, cols], pairs_hi[0:n, f, :], pairs_lo[0:n, f, :])

            def terms2(m, c):
                cols, x = slice(c * H2 + m * 128, c * H2 + (m + 1) * 128), slice(c * HALF, (c + 1) * HALF)
                return three(w2_hi[:, cols], w2_lo[:, cols], h1_hi[:, x], h1_lo[:, x])

            def layer1(q, m):
                if m == 0:
                    misc_drained(q, LAYER1)
                    pe.wait_ge(split_lo, NJ)
                    pe.wait_ge(dense_split, q + 1)
                i = LAYER1 + m // 2
                ps = misc_bank(q, i) if m % 2 == 0 else misc_ps[i % 2]
                mm = product(ps[:, m % 2 * HALF:(m % 2 + 1) * HALF],
                             [term for f in range(FCH + 1) for term in terms1(m, f)])
                if m % 2:
                    mm.then_inc(misc_full, 1)

            def layer2(q, m, first, last):
                if m == 0:
                    pe.wait_ge(h1_ready, M1 * (q + 1))
                    misc_bank(q, LAYER2)
                mm = product(misc_ps[LAYER2 % 2][:, m * HALF:(m + 1) * HALF],
                             [term for c in range(first, last) for term in terms2(m, c)],
                             start=(first == 0), stop=(last == M1))
                if m == M2 - 1 and last == M1:
                    mm.then_inc(misc_full, 1)

            def layer3(q):
                misc_drained(q, LAYER3)
                final(misc_bank(q, LAYER3)).then_inc(misc_full, 1)

            def final(ps):
                for a in range(2):
                    for c in range(M2):
                        mm = nc.tensor.matmul(ps[:, a:a + 1], h2[:, c, a * 128:(a + 1) * 128], w3s[:, c:c + 1],
                                              start=(c == 0), stop=(c == M2 - 1))
                return mm

            def half(k, kind):
                first = kind == "first"
                q = None if first else k - 1
                for n in range(4):
                    hot(k, n, first)
                    if not first:
                        back(q, n)
                parts = (0, 2), (2, 4), (4, GR)
                if first:
                    for n in range(4, NH):
                        hot(k, n, first)
                        turn(k, 0, *parts[n - 4], kind)
                    for e in range(NE):
                        extra(k, e, kind)
                        if e == 0:
                            turn(k, 0, *parts[2], kind)
                else:
                    hot(k, 4, first)
                    pair(q, 0)
                    pair(q, 1)
                    hot(k, 5, first)
                    for e in range(extras(kind)):
                        extra(k, e, kind)
                    for m in range(M1):
                        if m < len(parts):
                            turn(k, 0, *parts[m], kind)
                        layer1(q, m)
                if kind != "rest":
                    pe.wait_ge(extra_in, k + 1)
                gram(k, 0)
                turn(k, 1, 0, 2, kind)
                if not first:
                    layer2(q, 0, 0, M1)
                turn(k, 1, 2, 4, kind)
                if not first:
                    layer2(q, 1, 0, 1)
                turn(k, 1, 4, GR, kind)
                if not first:
                    layer2(q, 1, 1, M1)
                gram(k, 1)
                if not first:
                    layer3(q)

            pe.wait_ge(s_ident, 2)
            half(0, "first")
            pe.wait_ge(s_consts, 48)
            with pe.Fori(1, MORE) as k:
                half(k, "more")
            with pe.Fori(MORE, NHALF) as k:
                half(k, "rest")

            pe.wait_ge(dots_v, 2 * GB * NHALF + 2)
            pe.wait_ge(dots_a, 2 * GB * NHALF + 2)
            misc_drained(NHALF - 1, 0)
            for i, ps in enumerate(END_BACK):
                back_into(ps, i).then_inc(end_full, 1)
            pe.wait_ge(dense_split, NHALF)
            for m in range(M1):
                product(END_LAYER1[m], terms1(m, 0), stop=False)
            pe.wait_ge(end_v, 2)
            pe.wait_ge(end_a, 2)
            for i, ps in enumerate(END_PAIR):
                pair_into(ps, i).then_inc(end_full, 1)
            pe.wait_ge(end_hi, 1)
            for m in range(M1):
                product(END_LAYER1[m], terms1(m, 1)[:2] + terms1(m, 2)[:2], start=False, stop=False)
            pe.wait_ge(end_lo, 2)
            for m in range(M1):
                product(END_LAYER1[m], terms1(m, 3) + terms1(m, 1)[2:] + terms1(m, 2)[2:], start=False)\
                    .then_inc(end_full, 1)
            for c in range(M1):
                for part in range(2):
                    pe.wait_ge((end_hi, end_lo)[part], 2 + c + 1)
                    for m in range(M2):
                        terms = terms2(m, c)[2:] if part else terms2(m, c)[:2]
                        mm = product(END_LAYER2[m], terms, start=(c == 0 and not part), stop=(c == M1 - 1 and part == 1))
                        if c == M1 - 1 and part:
                            mm.then_inc(end_full, 1)
            pe.wait_ge(end_v, END_H2)
            pe.wait_ge(end_a, END_H2)
            final(END_LAYER3).then_inc(end_full, 1)

        def turn_copy(eng, copy, k, t, g, kind):
            u = t * GR + g
            eng.wait_ge(turn_full, 2 * GR * k + u + 1)
            w = len(turned_tables(g, kind))
            v = turn_ps[u % 2][:, 0:w * 128].rearrange("d (f s j) -> d j s f", f=w, s=SPG)
            copy(rows(t, 1 + TGROUPS[g][0], w), v).then_inc(turned_v if TURNS[u] == "v" else turned_a, 1)

        def misc_wait(eng, q, i):
            eng.wait_ge(misc_full, USES * q + i + 1)

        def back_out(eng, copy, q, i):
            misc_wait(eng, q, i)
            pairs_from(copy, misc_ps[i % 2], i).then_inc(misc_v if DRAINS[i] == "v" else misc_a, 1)

        def pairs_from(copy, ps, i):
            cps = range(4 * i, min(4 * i + 4, CPAIRS))
            for m, cp in enumerate(cps):
                v = ps[:, m * 128:(m + 1) * 128].rearrange("g (s r) -> g s r", s=SPG)
                at = first_merged(cp)
                copy(pairs[:, :, at:at + width(cp)], v[:, :, 2 * cp + 2:2 * cp + 2 + width(cp)])
            v = ps[0:GPH, 8 * i + 1:8 * i + 2]
            at = MERGED + 4 * i
            v = bass.AP(v.tensor, v.offset, [v.ap[0], [ROWS, SPG], [128 + 2, len(cps)]])
            return copy(pairs[0:GPH, :, at:at + len(cps)], v)

        def pair_bank(i, ps=None):
            ps = ps or misc_ps[(PAIR + i) % 2]
            if i == 0:
                return (ps[:, :].rearrange("p (s f g) -> p f s g", s=SPG, f=2),
                        *(x[:, 0:2, :].rearrange("p f (s g) -> p f s g", s=SPG) for x in (pairs_hi, pairs_lo)))
            return ps[0:FK[2], GPH:GPH + HALF], pairs_hi[0:FK[2], 2, :], pairs_lo[0:FK[2], 2, :]

        @block.scalar
        def _(act):
            def copy(out, in_):
                return nc.scalar.activation(out, in_, ACT.Copy)

            def split(j):
                data = staged(act, j)
                copy(jobs[j][3], data).then_inc(split_hi, 1)

            def hot_out(k, b):
                w = min(2, NH - 2 * b)
                act.wait_ge(hot_done, NH * k + 2 * b + w)
                for t in range(2):
                    v = hot_ps[b % 2][:, 0:w * HALF].rearrange("d (f t j s) -> d t j s f", f=w, t=2, j=JT)
                    out = copy(rows(t, 1 + NG + 2 * b, w), v[:, t])
                out.then_inc(hot_in, 1)

            def extra_out(k, kind):
                act.wait_ge(extra_done, extras_through(kind, k))
                for e in range(extras(kind)):
                    n = NH + e
                    for t in range(2):
                        v = hot_ps[n // 2 % 2][:, n % 2 * HALF:(n % 2 + 1) * HALF].rearrange("d (t j s) -> d t j s", t=2, j=JT)
                        out = copy(rows(t, NG - e, 1).rearrange("d j s r -> d j (s r)"), v[:, t])
                out.then_inc(extra_in, 1)

            def turn_out(k, t, first, last, kind):
                for g in range(first, last):
                    if TURNS[t * GR + g] == "a":
                        turn_copy(act, copy, k, t, g, kind)

            def dots_out(k, t, between={}):
                for b in range(GB):
                    if b in between:
                        between[b]()
                    act.wait_ge(dots_full, 2 * GB * k + t * GB + b + 1)
                    for s in (2, 3):
                        out = copy(dots_part(t, b, s), dots_bank(b, s))
                    out.then_inc(dots_a, 1)

            def pair_hi(q, i):
                misc_wait(act, q, PAIR + i)
                ps, high, low = pair_bank(i)
                copy(high, ps).then_inc(pairs_hi_ready, 1)

            def layer1_out(q, i):
                misc_wait(act, q, LAYER1 + i)
                for m in (2 * i, 2 * i + 1):
                    out = nc.scalar.activation(h1[:, m * HALF:(m + 1) * HALF],
                                               misc_ps[(LAYER1 + i) % 2][:, m % 2 * HALF:(m % 2 + 1) * HALF],
                                               ACT.Relu, bias=b1s[:, m:m + 1])
                out.then_inc(misc_a, 1)

            def layer1_hi(q, i):
                act.wait_ge(misc_a, DRAINS.count("a") * q + drained_before(LAYER1 + i + 1)[1] + 1)
                part = slice(2 * i * HALF, (2 * i + 2) * HALF)
                copy(h1_hi[:, part], h1[:, part]).then_inc(h1_hi_ready, 1)

            def layer2_out(q):
                misc_wait(act, q, LAYER2)
                for m in range(M2):
                    out = nc.scalar.activation(h2[:, m, :], misc_ps[LAYER2 % 2][:, m * HALF:(m + 1) * HALF],
                                               ACT.Relu, bias=b2s[:, m:m + 1])
                out.then_inc(misc_a, 1)

            def dense_hi_out(k):
                act.wait_ge(s_dense, 16 * (k + 1))
                copy(dense_hi[:, :], dense[:, :]).then_inc(dense_split_hi, 1)

            def half(k, kind):
                first = kind == "first"
                q = None if first else k - 1
                for n in range(4):
                    if first and n == 3:
                        split(4)
                        split(5)
                    if n % 2:
                        hot_out(k, n // 2)
                    if not first:
                        back_out(act, copy, q, n)
                if first:
                    for j in range(6, TJ):
                        split(j)
                    turn_out(k, 0, 0, 2, kind)
                    hot_out(k, 2)
                    turn_out(k, 0, 2, 4, kind)
                    split(TJ)
                    turn_out(k, 0, 4, GR, kind)
                    split(TJ + 1)
                    extra_out(k, kind)
                    act.wait_ge(split_lo, TJ)
                else:
                    pair_hi(q, 0)
                    pair_hi(q, 1)
                    hot_out(k, 2)
                    if extras(kind):
                        extra_out(k, kind)
                    turn_out(k, 0, 0, 4, kind)
                    layer1_out(q, 0)
                    turn_out(k, 0, 4, GR, kind)
                    layer1_hi(q, 0)
                    layer1_out(q, 1)
                dots_out(k, 0, {1: lambda: first or layer1_hi(q, 1), 3: lambda: first and split(TJ + 2),
                                4: lambda: dense_hi_out(k)})
                turn_out(k, 1, 0, GR, kind)
                if first:
                    split(FOLD)
                if not first:
                    layer2_out(q)
                dots_out(k, 1)

            for j in range(4):
                split(j)
            half(0, "first")
            act.wait_ge(s_consts, 48)
            with act.Fori(1, MORE) as k:
                half(k, "more")
            with act.Fori(MORE, NHALF) as k:
                half(k, "rest")

            def h1_hi_end(m):
                part = slice(m * HALF, (m + 1) * HALF)
                act.wait_ge((end_a, end_v)[m % 2], END_H1 + m // 2 + 1)
                copy(h1_hi[:, part], h1[:, part]).then_inc(end_hi, 1)

            for i in (0, 2):
                act.wait_ge(end_full, i + 1)
                pairs_from(copy, END_BACK[i], i).then_inc(end_a, 1)
            for i in range(2):
                act.wait_ge(end_full, 4 + i + 1)
                ps, high, low = pair_bank(i, END_PAIR[i])
                copy(high, ps).then_inc(end_hi, 1)
            for m in (0, 2):
                act.wait_ge(end_full, 6 + m + 1)
                nc.scalar.activation(h1[:, m * HALF:(m + 1) * HALF], END_LAYER1[m], ACT.Relu, bias=b1s[:, m:m + 1])\
                  .then_inc(end_a, 1)
                h1_hi_end(m)
                h1_hi_end(m + 1)
            act.wait_ge(end_full, 11)
            nc.scalar.activation(h2[:, 0, :], END_LAYER2[0], ACT.Relu, bias=b2s[:, 0:1]).then_inc(end_a, 1)

        @block.vector
        def _(dve):
            def copy(out, in_):
                return nc.vector.tensor_copy(out, in_)

            def rest(out, full, high):
                return nc.vector.tensor_tensor(out, full, high, ALU.subtract)

            def split(j):
                data = staged(dve, j)
                dve.wait_ge(split_hi, j + 1)
                rest(jobs[j][4], data, jobs[j][3]).then_inc(split_lo, 1)

            def stage(t, tile):
                copy(index[:, t, :], ids_sb[:, bass.ds(tile, 1), :].rearrange("p a f -> p (a f)"))\
                    .then_inc(index_ready[t], 1)

            def stage_next(k, t):
                dve.wait_ge(turn_full, 2 * GR * k + GR * (t + 1))
                stage(t, 2 * k + t + 2)

            def one_hot(n, chunks=range(HOT_CH)):
                ids = ids_cast[0:HOT_K, n * HALF:(n + 1) * HALF]
                for c in chunks:
                    out = nc.vector.tensor_scalar(onehot[0:HOT_K, n % UNITS, c, :], ids, row_id[0:HOT_K, c:c + 1], None,
                                                  ALU.is_equal)
                if c == HOT_CH - 1:
                    out.then_inc(onehot_ready, 1)

            def one_hot_extra(k, e):
                dve.wait_ge(s_cast_extra[e], 16 * (k + 1))
                dve.wait_ge(hot_done, NH * k + NH + e - UNITS + 1)
                for c in range(HOT_CH):
                    out = nc.vector.tensor_scalar(onehot[0:HOT_K, (NH + e) % UNITS, c, :], ids_cast_extra[0:HOT_K, e, :],
                                                  row_id[0:HOT_K, c:c + 1], None, ALU.is_equal)
                out.then_inc(extra_ready, 1)

            def one_hot_again(k, n):
                dve.wait_ge(hot_done, NH * k + n - UNITS + 1)
                one_hot(n)

            def dense_rows(k):
                dve.wait_ge(s_dense, 16 * (k + 1))
                for t in range(2):
                    v = dense[:, :].rearrange("d (s t j) -> d t j s", s=SPG, t=2)
                    out = copy(rows(t, 0, 1).rearrange("d j s r -> d j (s r)"), v[:, t])
                out.then_inc(dense_in, 1)

            def dots_out(k, t, between={}, ahead={}):
                for b in range(GB):
                    if b in between:
                        between[b]()
                    dve.wait_ge(dots_full, 2 * GB * k + t * GB + b + 1)
                    for s in (0, 1):
                        out = copy(dots_part(t, b, s), dots_bank(b, s))
                    out.then_inc(dots_v, 1)
                    if b in ahead:
                        one_hot_ahead(*ahead[b])

            def one_hot_ahead(first, count):
                for i in range(first, first + count):
                    one_hot(i // HOT_CH, [i % HOT_CH])

            def pair_lo(q, i):
                dve.wait_ge(pairs_hi_ready, 2 * q + i + 1)
                ps, high, low = pair_bank(i)
                rest(low, ps, high).then_inc(misc_v, 1)

            def h1_lo_out(q, i):
                dve.wait_ge(h1_hi_ready, 2 * q + i // 2 + 1)
                part = slice(i * HALF, (i + 1) * HALF)
                rest(h1_lo[:, part], h1[:, part], h1_hi[:, part]).then_inc(h1_ready, 1)

            def dense_lo_out(k):
                dve.wait_ge(dense_split_hi, k + 1)
                rest(dense_lo[:, :], dense[:, :], dense_hi[:, :]).then_inc(dense_split, 1)

            def result(q):
                misc_wait(dve, q, LAYER3)
                copy(ys[:, bass.ds(2 * q, 2)], misc_ps[LAYER3 % 2][:, 0:2]).then_inc(misc_v, 1)

            def half(k, kind):
                first = kind == "first"
                q = None if first else k - 1
                dense_rows(k)
                for n in range(UNITS, NH):
                    one_hot_again(k, n)
                    if first:
                        split(n)
                for e in range(extras(kind)):
                    if first:
                        split(NH + e)
                    one_hot_extra(k, e)
                if not first:
                    pair_lo(q, 0)
                    pair_lo(q, 1)
                if first:
                    split(TJ)
                    dve.wait_ge(s_ids, 16)
                stage_next(k, 0)
                if not first:
                    for i in range(2):
                        h1_lo_out(q, i)
                dve.wait_ge(s_cast[0], 16 * (k + 2))
                dve.wait_ge(hot_done, NH * (k + 1))
                if first:
                    split(TJ + 1)
                if extras(kind):
                    dve.wait_ge(extra_done, extras_through(kind, k))
                dots_out(k, 0, {3: lambda: split(TJ + 2)} if first else {2: lambda: h1_lo_out(q, 2), 3: lambda: h1_lo_out(q, 3)},
                         {b: (b - 4, 1) for b in range(4, GB)})
                if first:
                    dve.wait_ge(s_raw[jobs[FOLD][0]], 16 * sum(job[0] == jobs[FOLD][0] for job in jobs))
                    v = raw[jobs[FOLD][0]]
                    nc.vector.tensor_tensor(v[:, 0:H1], v[:, 0:H1], v[:, H1:2 * H1], ALU.add).then_inc(s_fold, 1)
                for g in range(GR):
                    if TURNS[GR + g] == "v":
                        turn_copy(dve, copy, k, 1, g, kind)
                        if g == 1:
                            one_hot_ahead(4, 4)
                            dense_lo_out(k)
                stage_next(k, 1)
                if first:
                    split(FOLD)
                    dve.wait_ge(split_lo, NJ)
                    nc.vector.memset(pairs[:, :, MERGED + CPAIRS:POS], 0.0)
                dots_out(k, 1, {}, {b: (8 + 2 * b, 2) for b in range(GB)})
                if not first:
                    result(q)

            nc.vector.memset(rows(0, SLOTS, ROWS - SLOTS), 0.0).then_inc(hot_in, 1)
            nc.vector.memset(rows(1, SLOTS, ROWS - SLOTS), 0.0).then_inc(hot_in, 1)
            nc.vector.memset(ids_sb[:, 2 * NHALF:, :], 0).then_inc(dots_v, 2)
            nc.vector.memset(scrap[:, 0:1], 0.0).then_inc(dots_a, 2)
            nc.vector.memset(scrap[:, 1:2], 0.0).then_inc(misc_v, 1)
            nc.vector.memset(scrap[:, 2:3], 0.0).then_inc(misc_a, 1)
            dve.wait_ge(s_rowid, 1)
            copy(row_id[:, :], row_id_i[:, :]).then_inc(s_rowid_f, 1)
            dve.wait_ge(s_rowid_f, 1)
            for n in range(UNITS):
                dve.wait_ge(s_cast_first if n == 0 else s_cast[0], 16)
                one_hot(n)
                split(n)
            dve.wait_ge(s_cast[1], 16)
            half(0, "first")
            with dve.Fori(1, MORE) as k:
                dve.wait_ge(s_cast[1], 16 * (k + 1))
                half(k, "more")
            with dve.Fori(MORE, NHALF) as k:
                dve.wait_ge(s_cast[1], 16 * (k + 1))
                half(k, "rest")

            def h1_lo_end(m):
                part = slice(m * HALF, (m + 1) * HALF)
                dve.wait_ge(end_hi, 2 + m + 1)
                rest(h1_lo[:, part], h1[:, part], h1_hi[:, part]).then_inc(end_lo, 1)

            def relu(out, ps, bias):
                return nc.vector.tensor_scalar(out, ps, bias, 0.0, ALU.add, ALU.max)

            for i in (1, 3):
                dve.wait_ge(end_full, i + 1)
                pairs_from(copy, END_BACK[i], i).then_inc(end_v, 1)
            for i in range(2):
                dve.wait_ge(end_hi, i + 1)
                ps, high, low = pair_bank(i, END_PAIR[i])
                rest(low, ps, high).then_inc(end_lo, 1)
            for m in (1, 3):
                dve.wait_ge(end_full, 6 + m + 1)
                relu(h1[:, m * HALF:(m + 1) * HALF], END_LAYER1[m], b1s[:, m:m + 1]).then_inc(end_v, 1)
                h1_lo_end(m - 1)
                h1_lo_end(m)
            dve.wait_ge(end_full, 12)
            relu(h2[:, 1, :], END_LAYER2[1], b2s[:, 1:2]).then_inc(end_v, 1)
            dve.wait_ge(end_full, 13)
            copy(ys[:, 2 * (NHALF - 1):], END_LAYER3[:, 0:2]).then_inc(end_v, 1)


def kernel(**inputs):
    import numpy as _np
    import concourse.bacc as _bacc
    from concourse import mybir as _mybir
    from concourse.bass_utils import run_bass_kernel_spmd as _run

    a = {name: _np.asarray(v) for name, v in inputs.items()}
    w1 = a["W_top1"]

    def weight_rows(found):
        rows = []
        for c, r in found:
            if c == 0:
                rows.append(D + ORDER[r - 1])
            else:
                f, g = sorted((ORDER[c - 1], ORDER[r - 1]))
                rows.append(D + TABLES + f * (TABLES - 1) - f * (f - 1) // 2 + g - f - 1)
        return w1[rows]

    even, odd = ([(c + side, r) for c in range(0, COLS, 2) for r in range(c + 2, SLOTS)] for side in (0, 1))
    even += [(c, c + 1) for c in range(0, COLS, 2)]
    w1_pairs = [weight_rows(even[:128]), weight_rows(odd[:128]), weight_rows(even[128:]),
                _np.zeros((POS - len(even), H1), w1.dtype), weight_rows(odd[128:])]
    ids = a["ids"].reshape(NHALF // 2, SPG, 2, 2, JT, TABLES)
    ids_tiles = ids.transpose(1, 4, 0, 2, 3, 5).reshape(TILE, 2 * NHALF, TABLES)
    ids_hot = ids[..., HOT].transpose(0, 2, 5, 3, 4, 1).reshape(NHALF, NH * HALF)
    dense = a["r_dense_features"].reshape(NHALF // 2, SPG, 2, GPH, D).transpose(0, 2, 4, 1, 3).reshape(NHALF, D, HALF)
    arrays = {
        "ids_tiles": ids_tiles,
        "ids_hot": _np.concatenate([ids_hot, ids_hot[:2]]),
        "ids_extra": ids[..., EXTRA].transpose(5, 0, 2, 3, 4, 1).reshape(NE, BATCH),
        "dense_t": _np.concatenate([dense, dense[:1]]),
        "w1_dense": _np.concatenate([w1[:D], w1[-D:]]),
        "w1_pairs": _np.concatenate(w1_pairs),
        "b1": a["b_top1"].reshape(-1, 128).T,
        "w2": a["W_top2"],
        "b2": a["b_top2"].reshape(-1, 128).T,
        "w3": a["W_top3"].reshape(-1, 128).T,
    }
    arrays.update({f"tbl_{t}": a[f"tbl_{t}"] for t in range(TABLES)})
    nc = _bacc.Bacc("TRN2", target_bir_lowering=False, num_devices=1)
    h = {}
    for name in arrays:
        arrays[name] = _np.ascontiguousarray(arrays[name])
        h[name] = nc.dram_tensor(name, arrays[name].shape, _mybir.dt.from_np(arrays[name].dtype), kind="ExternalInput").ap()
    y = nc.dram_tensor("y", (128, NHALF * 2), _mybir.dt.float32, kind="ExternalOutput").ap()
    build(nc, h["ids_tiles"], h["ids_hot"], h["ids_extra"], h["dense_t"], [h[f"tbl_{t}"] for t in range(TABLES)], h["w1_dense"],
          h["w1_pairs"], h["b1"], h["w2"], h["b2"], h["w3"], y)
    r = _run(nc, [arrays], core_ids=[0])
    out = r.results[0]["y"].reshape(2, GPH, NHALF // 2, 2, 2)
    return _np.ascontiguousarray(out.transpose(2, 4, 0, 3, 1)).reshape(BATCH, 1)
```
